# Optimizing a Trainium2 kernel written in Bass

```python
import numpy as np
import jax
import jax.numpy as jnp

def _softmax(x, axis=-1):
    return jax.nn.softmax(x, axis=axis)

def _gelu(x):
    return jax.nn.gelu(x, approximate=True)

def _silu(x):
    return jax.nn.silu(x)

def _sigmoid(x):
    return jax.nn.sigmoid(x)

def _layernorm(x, axis=-1, eps=1e-05):
    m = jnp.mean(x, axis=axis, keepdims=True)
    v = jnp.var(x, axis=axis, keepdims=True)
    return (x - m) / jnp.sqrt(v + eps)

def _scatter_add(tgt, idx, src, axis=0):
    return tgt.at[idx].add(src)

def _segment_sum(src, seg, n):
    return jax.ops.segment_sum(src, seg, n)
kernel_name = 'mk_seq_preln_d2_jaxref_r8_19a43b'

def setup_inputs(seed: int=0):
    np.random.seed(seed)
    _w = jnp.asarray

    def _L0_attn_setup():
        import jax, jax.numpy as jnp
        import numpy as np
        N_HEAD = 16
        CHUNK = 128
        N_EMBD = 128
        BATCH, SEQ = (1, 256)

        def _titans_forward(x, Wq, Wk, Wv, Wproj, alpha_raw, beta_raw):
            B, T, C = x.shape
            H = N_HEAD
            D = C // H
            CS = CHUNK
            NC = T // CS

            def proj(W):
                return jnp.einsum('btc,oc->bto', x, W).reshape(B, T, H, D).transpose(0, 2, 1, 3)
            q = proj(Wq)
            k = proj(Wk)
            v = proj(Wv)
            k = k / jnp.maximum(jnp.linalg.norm(k, axis=-1, keepdims=True), 1e-12)
            alpha = (jax.nn.sigmoid(alpha_raw) * 0.5).reshape(1, H, 1, 1, 1)
            beta = (jax.nn.sigmoid(beta_raw) * 0.5).reshape(1, H, 1, 1, 1)

            def tchunks(a):
                return a.reshape(B, H, NC, CS, D).transpose(3, 0, 1, 2, 4)
            qs, ks, vs = (tchunks(q), tchunks(k), tchunks(v))

            def op_step(carry, xs):
                A, Bm = carry
                kt, vt = xs
                kouter = kt[..., None, :]
                Ak = jnp.einsum('bhnde,bhne->bhnd', A, kt)
                Bk = jnp.einsum('bhnde,bhne->bhnd', Bm, kt)
                A = A - alpha * (Ak[..., None] * kouter)
                Bm = Bm - alpha * (Bk[..., None] * kouter) + beta * (vt[..., None] * kouter)
                return ((A, Bm), None)
            I = jnp.broadcast_to(jnp.eye(D, dtype=x.dtype), (B, H, NC, D, D))
            Z = jnp.zeros((B, H, NC, D, D), x.dtype)
            (A_ch, B_ch), _ = jax.lax.scan(op_step, (I, Z), (ks, vs))

            def chunk_step(M, AB):
                Ai, Bi = AB
                Mn = jnp.einsum('bhde,bhef->bhdf', M, Ai) + Bi
                return (Mn, M)
            A_cm = A_ch.transpose(2, 0, 1, 3, 4)
            B_cm = B_ch.transpose(2, 0, 1, 3, 4)
            M_final, M_starts = jax.lax.scan(chunk_step, jnp.zeros((B, H, D, D), x.dtype), (A_cm, B_cm))
            M0 = M_starts.transpose(1, 2, 0, 3, 4)

            def out_step(M, xs):
                qt, kt, vt = xs
                yt = jnp.einsum('bhnde,bhne->bhnd', M, qt)
                Mk = jnp.einsum('bhnde,bhne->bhnd', M, kt)
                kouter = kt[..., None, :]
                M = M - alpha * (Mk[..., None] * kouter) + beta * (vt[..., None] * kouter)
                return (M, yt)
            _, ys = jax.lax.scan(out_step, M0, (qs, ks, vs))
            y = ys.transpose(1, 2, 3, 0, 4).reshape(B, H, T, D)
            y = y.transpose(0, 2, 1, 3).reshape(B, T, C)
            y = jnp.einsum('btc,oc->bto', y, Wproj)
            return (y, M_final)

        def _reference_tuple_inner(x, Wq, Wk, Wv, Wproj, alpha_raw, beta_raw):
            return _titans_forward(x, Wq, Wk, Wv, Wproj, alpha_raw, beta_raw)
        key = jax.random.key(seed)
        ks = jax.random.split(key, 7)
        s = 0.02
        return {'x': jax.random.normal(ks[0], (BATCH, SEQ, N_EMBD), jnp.float32), 'Wq': jax.random.normal(ks[1], (N_EMBD, N_EMBD), jnp.float32) * s, 'Wk': jax.random.normal(ks[2], (N_EMBD, N_EMBD), jnp.float32) * s, 'Wv': jax.random.normal(ks[3], (N_EMBD, N_EMBD), jnp.float32) * s, 'Wproj': jax.random.normal(ks[4], (N_EMBD, N_EMBD), jnp.float32) * s, 'alpha_raw': jax.random.normal(ks[5], (N_HEAD,), jnp.float32), 'beta_raw': jax.random.normal(ks[6], (N_HEAD,), jnp.float32)}
    _L0_attn_in = _L0_attn_setup()

    def _L0_ffn_setup():
        import jax, jax.numpy as jnp
        import numpy as np
        E, K, D, H = (8, 2, 128, 256)
        B, S = (1, 128)

        def _grouped_swiglu(x_sorted, counts, w1, w2, w3):
            if hasattr(jax.lax, 'ragged_dot'):
                gs = counts.astype(jnp.int32)
                h = jax.nn.silu(jax.lax.ragged_dot(x_sorted, w1, gs)) * jax.lax.ragged_dot(x_sorted, w3, gs)
                return jax.lax.ragged_dot(h, w2, gs)
            pos = jnp.arange(x_sorted.shape[0])
            eid = jnp.searchsorted(jnp.cumsum(counts), pos, side='right')
            out = jnp.zeros((x_sorted.shape[0], w2.shape[-1]), x_sorted.dtype)
            for e in range(w1.shape[0]):
                xm = jnp.where((eid == e)[:, None], x_sorted, 0.0)
                he = jax.nn.silu(xm @ w1[e]) * (xm @ w3[e])
                out = out + he @ w2[e]
            return out
        key = jax.random.key(seed)
        k0, k1, k2, k3, k4 = jax.random.split(key, 5)
        sD = 1.0 / np.sqrt(D)
        sH = 1.0 / np.sqrt(H)
        return {'hidden_states': jax.random.normal(k0, (B, S, D), jnp.float32), 'gate_w': jax.random.normal(k1, (E, D), jnp.float32) * sD, 'w1': jax.random.normal(k2, (E, D, H), jnp.float32) * sD, 'w2': jax.random.normal(k3, (E, H, D), jnp.float32) * sH, 'w3': jax.random.normal(k4, (E, D, H), jnp.float32) * sD}
    _L0_ffn_in = _L0_ffn_setup()

    def _L1_attn_setup():
        import jax, jax.numpy as jnp
        import numpy as np
        D_MODEL, H, DK, DV = (128, 16, 64, 64)
        key = jax.random.key(seed)
        ks = jax.random.split(key, 9)
        s = lambda fan_in: 1.0 / np.sqrt(fan_in)
        return {'x': jax.random.normal(ks[0], (2, 256, D_MODEL), dtype=jnp.float32), 'Wq': jax.random.uniform(ks[1], (D_MODEL, H * DK), jnp.float32, -s(D_MODEL), s(D_MODEL)), 'bq': jax.random.uniform(ks[2], (H * DK,), jnp.float32, -s(D_MODEL), s(D_MODEL)), 'Wk': jax.random.uniform(ks[3], (D_MODEL, DK), jnp.float32, -s(D_MODEL), s(D_MODEL)), 'bk': jax.random.uniform(ks[4], (DK,), jnp.float32, -s(D_MODEL), s(D_MODEL)), 'Wv': jax.random.uniform(ks[5], (D_MODEL, DV), jnp.float32, -s(D_MODEL), s(D_MODEL)), 'bv': jax.random.uniform(ks[6], (DV,), jnp.float32, -s(D_MODEL), s(D_MODEL)), 'Wo': jax.random.uniform(ks[7], (H * DV, D_MODEL), jnp.float32, -s(H * DV), s(H * DV)), 'bo': jax.random.uniform(ks[8], (D_MODEL,), jnp.float32, -s(H * DV), s(H * DV))}
    _L1_attn_in = _L1_attn_setup()

    def _L1_ffn_setup():
        import jax, jax.numpy as jnp
        import numpy as np
        HIDDEN = 128
        INTER = 512
        key = jax.random.key(seed)
        k1, k2, k3, k4, k5 = jax.random.split(key, 5)
        hidden_states = jax.random.normal(k1, (4, 256, HIDDEN), dtype=jnp.float32)
        W1 = jax.random.normal(k2, (HIDDEN, INTER), dtype=jnp.float32) * (1.0 / np.sqrt(HIDDEN))
        b1 = jax.random.normal(k3, (INTER,), dtype=jnp.float32) * 0.02
        W2 = jax.random.normal(k4, (INTER, HIDDEN), dtype=jnp.float32) * (1.0 / np.sqrt(INTER))
        b2 = jax.random.normal(k5, (HIDDEN,), dtype=jnp.float32) * 0.02
        return {'hidden_states': hidden_states, 'W1': W1, 'b1': b1, 'W2': W2, 'b2': b2}
    _L1_ffn_in = _L1_ffn_setup()
    _d = {'L0_attn_x': _L0_attn_in['x'], 'L0_attn_Wq': _L0_attn_in['Wq'], 'L0_attn_Wk': _L0_attn_in['Wk'], 'L0_attn_Wv': _L0_attn_in['Wv'], 'L0_attn_Wproj': _L0_attn_in['Wproj'], 'L0_attn_alpha_raw': _L0_attn_in['alpha_raw'], 'L0_attn_beta_raw': _L0_attn_in['beta_raw'], 'L0_ffn_gate_w': _L0_ffn_in['gate_w'], 'L0_ffn_w1': _L0_ffn_in['w1'], 'L0_ffn_w2': _L0_ffn_in['w2'], 'L0_ffn_w3': _L0_ffn_in['w3'], 'L1_attn_Wq': _L1_attn_in['Wq'], 'L1_attn_bq': _L1_attn_in['bq'], 'L1_attn_Wk': _L1_attn_in['Wk'], 'L1_attn_bk': _L1_attn_in['bk'], 'L1_attn_Wv': _L1_attn_in['Wv'], 'L1_attn_bv': _L1_attn_in['bv'], 'L1_attn_Wo': _L1_attn_in['Wo'], 'L1_attn_bo': _L1_attn_in['bo'], 'L1_ffn_W1': _L1_ffn_in['W1'], 'L1_ffn_b1': _L1_ffn_in['b1'], 'L1_ffn_W2': _L1_ffn_in['W2'], 'L1_ffn_b2': _L1_ffn_in['b2']}
    _x0 = _d['L0_attn_x']
    _d['L0_attn_x'] = jax.random.normal(jax.random.fold_in(jax.random.key(seed), 1), (1, 2048, 128), dtype=_x0.dtype)
    del _x0
    return _d

def reference(L0_attn_x, L0_attn_Wq, L0_attn_Wk, L0_attn_Wv, L0_attn_Wproj, L0_attn_alpha_raw, L0_attn_beta_raw, L0_ffn_gate_w, L0_ffn_w1, L0_ffn_w2, L0_ffn_w3, L1_attn_Wq, L1_attn_bq, L1_attn_Wk, L1_attn_bk, L1_attn_Wv, L1_attn_bv, L1_attn_Wo, L1_attn_bo, L1_ffn_W1, L1_ffn_b1, L1_ffn_W2, L1_ffn_b2):

    def _L0_attn_ref(x, Wq, Wk, Wv, Wproj, alpha_raw, beta_raw):
        import jax, jax.numpy as jnp
        import numpy as np
        N_HEAD = 16
        CHUNK = 128
        N_EMBD = 128
        BATCH, SEQ = (1, 256)

        def _titans_forward(x, Wq, Wk, Wv, Wproj, alpha_raw, beta_raw):
            B, T, C = x.shape
            H = N_HEAD
            D = C // H
            CS = CHUNK
            NC = T // CS

            def proj(W):
                return jnp.einsum('btc,oc->bto', x, W).reshape(B, T, H, D).transpose(0, 2, 1, 3)
            q = proj(Wq)
            k = proj(Wk)
            v = proj(Wv)
            k = k / jnp.maximum(jnp.linalg.norm(k, axis=-1, keepdims=True), 1e-12)
            alpha = (jax.nn.sigmoid(alpha_raw) * 0.5).reshape(1, H, 1, 1, 1)
            beta = (jax.nn.sigmoid(beta_raw) * 0.5).reshape(1, H, 1, 1, 1)

            def tchunks(a):
                return a.reshape(B, H, NC, CS, D).transpose(3, 0, 1, 2, 4)
            qs, ks, vs = (tchunks(q), tchunks(k), tchunks(v))

            def op_step(carry, xs):
                A, Bm = carry
                kt, vt = xs
                kouter = kt[..., None, :]
                Ak = jnp.einsum('bhnde,bhne->bhnd', A, kt)
                Bk = jnp.einsum('bhnde,bhne->bhnd', Bm, kt)
                A = A - alpha * (Ak[..., None] * kouter)
                Bm = Bm - alpha * (Bk[..., None] * kouter) + beta * (vt[..., None] * kouter)
                return ((A, Bm), None)
            I = jnp.broadcast_to(jnp.eye(D, dtype=x.dtype), (B, H, NC, D, D))
            Z = jnp.zeros((B, H, NC, D, D), x.dtype)
            (A_ch, B_ch), _ = jax.lax.scan(op_step, (I, Z), (ks, vs))

            def chunk_step(M, AB):
                Ai, Bi = AB
                Mn = jnp.einsum('bhde,bhef->bhdf', M, Ai) + Bi
                return (Mn, M)
            A_cm = A_ch.transpose(2, 0, 1, 3, 4)
            B_cm = B_ch.transpose(2, 0, 1, 3, 4)
            M_final, M_starts = jax.lax.scan(chunk_step, jnp.zeros((B, H, D, D), x.dtype), (A_cm, B_cm))
            M0 = M_starts.transpose(1, 2, 0, 3, 4)

            def out_step(M, xs):
                qt, kt, vt = xs
                yt = jnp.einsum('bhnde,bhne->bhnd', M, qt)
                Mk = jnp.einsum('bhnde,bhne->bhnd', M, kt)
                kouter = kt[..., None, :]
                M = M - alpha * (Mk[..., None] * kouter) + beta * (vt[..., None] * kouter)
                return (M, yt)
            _, ys = jax.lax.scan(out_step, M0, (qs, ks, vs))
            y = ys.transpose(1, 2, 3, 0, 4).reshape(B, H, T, D)
            y = y.transpose(0, 2, 1, 3).reshape(B, T, C)
            y = jnp.einsum('btc,oc->bto', y, Wproj)
            return (y, M_final)

        def _reference_tuple_inner(x, Wq, Wk, Wv, Wproj, alpha_raw, beta_raw):
            return _titans_forward(x, Wq, Wk, Wv, Wproj, alpha_raw, beta_raw)
        return _reference_tuple_inner(x, Wq, Wk, Wv, Wproj, alpha_raw, beta_raw)[0]

    def _L0_ffn_ref(hidden_states, gate_w, w1, w2, w3):
        import jax, jax.numpy as jnp
        import numpy as np
        E, K, D, H = (8, 2, 128, 256)
        B, S = (1, 128)

        def _grouped_swiglu(x_sorted, counts, w1, w2, w3):
            if hasattr(jax.lax, 'ragged_dot'):
                gs = counts.astype(jnp.int32)
                h = jax.nn.silu(jax.lax.ragged_dot(x_sorted, w1, gs)) * jax.lax.ragged_dot(x_sorted, w3, gs)
                return jax.lax.ragged_dot(h, w2, gs)
            pos = jnp.arange(x_sorted.shape[0])
            eid = jnp.searchsorted(jnp.cumsum(counts), pos, side='right')
            out = jnp.zeros((x_sorted.shape[0], w2.shape[-1]), x_sorted.dtype)
            for e in range(w1.shape[0]):
                xm = jnp.where((eid == e)[:, None], x_sorted, 0.0)
                he = jax.nn.silu(xm @ w1[e]) * (xm @ w3[e])
                out = out + he @ w2[e]
            return out
        x = hidden_states.reshape(-1, D)
        N = x.shape[0]
        scores = jax.nn.softmax(x @ gate_w.T, axis=-1)
        top_scores, sel = jax.lax.top_k(scores, K)
        sel_flat = sel.T.reshape(-1)
        scores_flat = top_scores.T.reshape(-1)
        order = jnp.argsort(sel_flat, stable=True)
        tok_sorted = order % N
        scores_sorted = scores_flat[order]
        counts = jnp.bincount(sel_flat, length=E)
        x_sorted = x[tok_sorted]
        y = _grouped_swiglu(x_sorted, counts, w1, w2, w3)
        weighted = y * scores_sorted[:, None]
        out = jnp.zeros((N, D), x.dtype).at[tok_sorted].add(weighted)
        return out.reshape(hidden_states.shape)

    def _L1_attn_ref(x, Wq, bq, Wk, bk, Wv, bv, Wo, bo):
        import jax, jax.numpy as jnp
        import numpy as np
        D_MODEL, H, DK, DV = (128, 16, 64, 64)
        B, S, _ = x.shape
        q = (x @ Wq + bq).reshape(B, S, H, DK)
        k = x @ Wk + bk
        v = x @ Wv + bv
        scores = jnp.einsum('bshd,btd->bhst', q, k) / np.sqrt(DK).astype(x.dtype)
        w = jax.nn.softmax(scores, axis=-1)
        out = jnp.einsum('bhst,btd->bshd', w, v).reshape(B, S, H * DV)
        return out @ Wo + bo

    def _L1_ffn_ref(hidden_states, W1, b1, W2, b2):
        import jax, jax.numpy as jnp
        import numpy as np
        HIDDEN = 128
        INTER = 512
        h = jax.nn.relu(jnp.einsum('bsh,hi->bsi', hidden_states, W1) + b1)
        return jnp.einsum('bsi,ih->bsh', h, W2) + b2
    x = L0_attn_x
    x = x + _L0_attn_ref(_layernorm(x, axis=-1), L0_attn_Wq, L0_attn_Wk, L0_attn_Wv, L0_attn_Wproj, L0_attn_alpha_raw, L0_attn_beta_raw)
    x = x + _L0_ffn_ref(_layernorm(x, axis=-1), L0_ffn_gate_w, L0_ffn_w1, L0_ffn_w2, L0_ffn_w3)
    x = x + _L1_attn_ref(_layernorm(x, axis=-1), L1_attn_Wq, L1_attn_bq, L1_attn_Wk, L1_attn_bk, L1_attn_Wv, L1_attn_bv, L1_attn_Wo, L1_attn_bo)
    x = x + _L1_ffn_ref(_layernorm(x, axis=-1), L1_ffn_W1, L1_ffn_b1, L1_ffn_W2, L1_ffn_b2)
    return x

_drawn_inputs = setup_inputs


def setup_inputs(seed=0):
    import zlib

    import numpy as np

    out = dict(_drawn_inputs(seed))
    spreads = {}
    factors = {'L0_attn_beta_raw': 2.89,
     'L1_attn_Wq': 5.647,
     'L1_attn_bq': 8.0,
     'L1_attn_Wk': 5.723,
     'L1_attn_bk': 64.0,
     'L1_attn_Wv': 4.857,
     'L1_attn_bo': 3.165,
     'L1_ffn_b1': 5.15,
     'L1_ffn_b2': 3.507,
     'L1_attn_bv': 2.794}
    for name, (base, spread) in spreads.items():
        noise = np.random.default_rng([zlib.crc32(name.encode()), seed]).standard_normal(out[name].shape)
        drawn = base * np.exp(spread * noise) if base else spread * noise
        out[name] = jnp.asarray(drawn.astype(out[name].dtype))
    for name, factor in factors.items():
        out[name] = (out[name] * factor).astype(out[name].dtype)
    return out
```

```python
from contextlib import ExitStack

import concourse.bass as bass
from concourse import mybir

ALU = mybir.AluOpType
ACT = mybir.ActivationFunctionType
AX = mybir.AxisListType
F32 = mybir.dt.float32
F16 = mybir.dt.float16

P = 128
T = 2048
NT = T // P
NB = 4
BT = T // NB
TPB = NT // NB
HEADS = 16
DH = P // HEADS
SUB = NT
NSUB = T // SUB
RG = 4
NRG = NSUB // RG
SLOTS = 4
EXPERTS, HID, TOPK = 8, 256, 2
DK = 64
FF = 512
KT = T // P
STEPS = KT // 2
MSPLIT = 64.0
EPS = 1e-5
MAX_CHUNKS = [3, 3, 3, 3, 2, 2, 0, 0]


FREE = {"a_masked": 2, "y_ready": 2, "act1_ready": 2, "hid_ready": 2, "down_added": 3, "p_ready": 2, "pv_done": 4,
          "pool_acc": 5, "tail_done": 1, "acc_read": 1, "mx_free": 2, "o_saved": 1, "wo_ready": 1, "wo_added": 1,
          "ff_ready": 4, "fo_added": 2, "m_psum": 12, "m_ready": 4}


class Steps:

    def __init__(self, engine, sem):
        self.engine, self.sem, self.count = engine, sem, 0

    def __call__(self, instruction):
        instruction.then_inc(self.sem, 1)
        self.count = self.count + 1
        self.engine.wait_ge(self.sem, self.count)


def build(nc, io, out):
    with ExitStack() as ctx:
        def sb(name, shape, dt=F32, scope=ctx):
            return scope.enter_context(nc.sbuf_tensor(name, shape, dt))

        def sem(name):
            return ctx.enter_context(nc.semaphore(name))

        x = sb("x", [P, NT, P])
        xn = sb("xn", [P, NT, P])
        xnT = sb("xnT", [P, T])
        work = sb("work", [P, NT, P])
        row_sum = sb("row_sum", [P, NT])
        mean = sb("mean", [P, NT])
        var = sb("var", [P, NT])
        rstd = sb("rstd", [P, NT])
        ident = sb("ident", [P, P])
        ident16 = sb("ident16", [P, P], F16)
        mask = sb("mask", [P, P])
        negmask = sb("negmask", [P, RG, P])
        eye4 = sb("eye4", [P, RG, P])
        ones = sb("ones", [P, 1])
        zeros16 = sb("zeros16", [DK, BT], F16)
        minus_half = sb("minus_half", [P, 2 * P])
        earlier = sb("earlier", [P, EXPERTS, EXPERTS])
        wqkv = sb("wqkv", [P, 3 * P])
        wproj = sb("wproj", [P, P])
        ab = sb("ab", [P, 2, HEADS])
        gate = sb("gate", [P, EXPERTS])
        wq = sb("wq", [P, HEADS * DK])
        bq = sb("bq", [DK, HEADS])
        wk2 = sb("wk2", [P, 2, DK])
        bk2 = sb("bk2", [P, 1])
        wv = sb("wv", [P, DK])
        bv = sb("bv", [P, DK])
        wo2 = sb("wo2", [P, HEADS, P])
        bo = sb("bo", [P, P])
        w1 = sb("w1", [P, FF])
        b1 = sb("b1", [P, FF // P])
        w2 = sb("w2", [P, FF // P, P])
        b2 = sb("b2", [P, P])

        a_scope = ExitStack()
        sa_ = lambda name, shape, dt=F32: sb(name, shape, dt, a_scope)
        kaq = sa_("kaq", [P, NT, 2, P])
        kv = sa_("kv", [P, NT, 2 * P])
        ukk = sa_("ukk", [P, NT, 3, P])
        ukt = sa_("ukt", [P, NT, HEADS, 2 * DH])
        dots = sa_("dots", [P, NT * HEADS])
        corr = sa_("corr", [P, HEADS * 2 * DH])
        kss = sa_("kss", [P, NT * HEADS])
        krn = sa_("krn", [P, NT * HEADS])
        sub = sa_("sub", [SUB, SLOTS, RG, 3 * P])
        amat = sa_("amat", [P, 2, RG, P])
        mst = sa_("mst", [P, RG, P])
        qT = sa_("qT", [P, NT, P])
        yT = sa_("yT", [P, NT, P])
        kn = ukk[:, :, 2, :]
        prod1 = work
        prod2 = kv
        a_scope.close()

        sbb = sb
        ew1 = sbb("ew1", [P, 2, HID])
        ew3 = sbb("ew3", [P, 2, HID])
        ew2 = sbb("ew2", [P, 2, HID // P, P])
        act1 = sbb("act1", [P, 2, BT])
        hidT = sbb("hidT", [P, 2, HID // P, BT])
        r1 = sbb("r1", [P, NT])
        probs = sbb("probs", [P, NT, EXPERTS])
        cmp_gt = sbb("cmp_gt", [P, NT, EXPERTS, EXPERTS])
        cmp_eq = sbb("cmp_eq", [P, NT, EXPERTS, EXPERTS])
        rank = sbb("rank", [P, NT, EXPERTS])
        gatew = sbb("gatew", [P, NT, EXPERTS])
        khh = sb("khh", [P, T], F16)
        klm = sb("klm", [DK + 2, T], F16)
        vt = sb("vt", [P, KT, DK])
        qhl = sb("qhl", [P, HEADS, BT], F16)
        qhm = sb("qhm", [DK + 2, HEADS, BT], F16)
        pr = sb("pr", [P, 4, 2, BT])
        acc = sb("acc", [P, 2, BT])
        tail = sb("tail", [P, 2, BT])
        keysum = sb("keysum", [P, BT])
        osb = sb("osb", [P, BT])
        cmax = sb("cmax", [P, TPB, NB])
        nmax = sb("nmax", [P, TPB])
        m16 = sb("m16", [P, TPB, 2], F16)
        rden = sb("rden", [P, TPB])
        ffT = sb("ffT", [P, 2, FF // P, BT])

        ps = ctx.enter_context(nc.psum_tensor("ps", [P, 8, BT], F32))

        def bank(b):
            return ps[:, b, :]

        MX, OB, SM = 4, 6, 7
        small16 = ps[:, SM, :].bitcast(F16)

        scratch = nc.dram_tensor("scratch", [T, 3 * P], F32, kind="Internal").ap()

        (x_in, w_in, consts, pool_step, dve_step, xn_ready, xnT_psum, xnT_ready, var_ready, rstd_ready,
         ab_exp, qkv_psum, qkv_ready, kss_ready, krn_ready, solved, ukk_ready, scratch_out, qo_ready,
         qo_psum, qo_sbuf, a_psum, a_masked, a_ready, m_psum, m_ready, y_psum, y_ready, proj_psum, x_added,
         gate_psum, shift_ready, gate_exp, up_psum, gt_psum, act1_ready, hid_ready, down_psum, down_added,
         kp_psum, kh_ready, kl_ready, vp_psum, v_ready, bo_added, q_psum, qh_ready, ql_ready, qm_copied,
         st_ready, p_ready, pv_done, pool_acc, tail_done, acc_read, keysum_ready, mx_ready, mx_free,
         max_step, rowmax_ready, tr_ready, t2_ready, o_saved, den_ready, den_read, wo_ready, wo_added,
         b2_added, ff_psum, ff_ready, fo_psum, fo_added, y_out, klm_ones) = (sem(n) for n in """
            x_in w_in consts pool_step dve_step xn_ready xnT_psum xnT_ready var_ready rstd_ready ab_exp
            qkv_psum qkv_ready kss_ready krn_ready solved ukk_ready scratch_out qo_ready qo_psum qo_sbuf a_psum
            a_masked a_ready m_psum m_ready y_psum y_ready proj_psum x_added gate_psum shift_ready gate_exp
            up_psum gt_psum act1_ready hid_ready down_psum down_added kp_psum kh_ready kl_ready vp_psum v_ready
            bo_added q_psum qh_ready ql_ready qm_copied st_ready p_ready pv_done pool_acc tail_done acc_read
            keysum_ready mx_ready mx_free max_step rowmax_ready tr_ready t2_ready o_saved den_ready den_read
            wo_ready wo_added b2_added ff_psum ff_ready fo_psum fo_added y_out klm_ones""".split())
        sub_in = [sem(f"sub_in{b}") for b in range(SLOTS)]
        ew_in = [sem(f"ew_in{b}") for b in range(2)]
        block = ctx.enter_context(nc.Block())

        xv = io["x"].rearrange("o (p i) c -> (o p) i c", p=P)
        ov = out.rearrange("o (p i) c -> (o p) i c", p=P)
        loads = [(wqkv[:, :], io["wqkv"]), (ab[:, 0, :], io["alpha"].partition_broadcast(P)),
                 (ab[:, 1, :], io["beta"].partition_broadcast(P)),
                 (wproj[:, :], io["wproj"]), (gate[:, :], io["gate"]), (wq[:, :], io["wq"]),
                 (bq[:, :], io["bq"]), (wk2[:, 0, :], io["wk"]), (wk2[:, 1, :], io["wk"]),
                 (bk2[0:DK, :], io["bk"]), (bk2[DK:2 * DK, :], io["bk"]), (wv[:, :], io["wv"]),
                 (bv[:, :], io["bv"].partition_broadcast(P)),
                 (wo2[0:DK, :, :], io["wo"].rearrange("(h d) m -> d h m", h=HEADS)),
                 (wo2[DK:2 * DK, :, :], io["wo"].rearrange("(h d) m -> d h m", h=HEADS)),
                 (bo[:, :], io["bo"].partition_broadcast(P)),
                 (w1[:, :], io["w1"]), (b1[:, :], io["b1"]),
                 (w2[:, :, :], io["w2"].rearrange("(j p) m -> p j m", p=P)),
                 (b2[:, :], io["b2"].partition_broadcast(P))]
        UP = 2 * NB
        NCH = TPB * NB
        ADDS = 5

        @block.sync
        def _(sp):
            sp.dma_start(x[:, :, :], xv).then_inc(x_in, 16)
            sp.wait_ge(ukk_ready, 2)
            scr = scratch.rearrange("(p i) c -> p i c", p=P)
            sp.dma_start(scr, ukk[:, :, :, :].rearrange("p i a c -> p i (a c)")).then_inc(scratch_out, 16)
            sp.wait_ge(scratch_out, 16)
            groups = scratch.rearrange("(q g i) c -> q i g c", g=RG, i=SUB)
            with sp.Fori(0, NRG // SLOTS) as it:
                for b in range(SLOTS):
                    sp.wait_ge(m_psum, (it * SLOTS + b - SLOTS + 1) * RG + FREE["m_psum"])
                    sp.dma_start(sub[:, b, :, :],
                                 groups[bass.ds(it * SLOTS + b, 1)].rearrange("o i g c -> (o i) g c")
                                 ).then_inc(sub_in[b], 16)
            sp.wait_ge(x_added, NB)

            def load_expert(e, s):
                loaded = ew_in[s]
                sp.dma_start(ew1[:, s, :], io["ew1"][bass.ds(e, 1)].rearrange("o d h -> (o d) h")).then_inc(loaded, 16)
                sp.dma_start(ew3[:, s, :], io["ew3"][bass.ds(e, 1)].rearrange("o d h -> (o d) h")).then_inc(loaded, 16)
                sp.dma_start(ew2[:, s, :, :],
                             io["ew2"][bass.ds(e, 1)].rearrange("o (j p) c -> (o p) j c", p=P)).then_inc(loaded, 16)

            load_expert(0, 0)
            load_expert(1, 1)
            with sp.Fori(1, EXPERTS // 2) as ep:
                for s in range(2):
                    sp.wait_ge(down_psum, ep * (2 * NB) - NB * (1 - s))
                    load_expert(ep * 2 + s, s)
            for b in range(NB):
                sp.wait_ge(fo_added, b + 1 + FREE["fo_added"])
                sp.dma_start(ov[:, TPB * b:TPB * (b + 1), :], x[:, TPB * b:TPB * (b + 1), :]).then_inc(y_out, 16)
            sp.wait_ge(y_out, 16 * NB)

        @block.gpsimd
        def _(pool):
            pool.sem_inc(pool_acc, FREE["pool_acc"])
            step = Steps(pool, pool_step)
            step(nc.gpsimd.memset(ident[:, :], 0.0))
            step(nc.gpsimd.affine_select(out=ident[:, :], in_=ident[:, :], compare_op=ALU.not_equal, fill=1.0,
                                         base=0, pattern=[[-1, P]], channel_multiplier=1))
            nc.gpsimd.tensor_copy(ident16[:, :], ident[:, :])
            for g in range(RG):
                nc.gpsimd.tensor_copy(eye4[:, g, :], ident[:, :])
            step(nc.gpsimd.memset(mask[:, :], 1.0))
            mask_v = mask[:, :].rearrange("p (h d) -> p h d", d=DH)
            step(nc.gpsimd.affine_select(out=mask_v, in_=mask_v, compare_op=ALU.is_ge, fill=0.0, base=0,
                                         pattern=[[-DH, HEADS], [0, DH]], channel_multiplier=1))
            step(nc.gpsimd.affine_select(out=mask_v, in_=mask_v, compare_op=ALU.is_ge, fill=0.0, base=DH - 1,
                                         pattern=[[DH, HEADS], [0, DH]], channel_multiplier=-1))
            for g in range(RG):
                nc.gpsimd.tensor_scalar(negmask[:, g, :], mask[:, :], -1.0, None, ALU.mult)
            nc.gpsimd.memset(ones[:, :], 1.0)
            nc.gpsimd.memset(zeros16[:, :], 0.0)
            nc.gpsimd.memset(minus_half[:, :], -0.5)
            step(nc.gpsimd.memset(earlier[:, :, :], 1.0))
            nc.gpsimd.affine_select(out=earlier[:, :, :], in_=earlier[:, :, :], compare_op=ALU.is_gt, fill=0.0, base=0,
                                    pattern=[[1, EXPERTS], [-1, EXPERTS]],
                                    channel_multiplier=0).then_inc(consts, 1)

            def rsqrt_rows(k):
                pool.wait_ge(var_ready, k)
                nc.gpsimd.tensor_tensor(rstd[:, :], var[:, :], minus_half[:, 0:NT],
                                        ALU.pow).then_inc(rstd_ready, 1)

            pool.wait_ge(consts, 1)
            rsqrt_rows(1)
            pool.wait_ge(kss_ready, 1)
            step(nc.gpsimd.tensor_tensor(krn[:, :], kss[:, :], minus_half[:, :], ALU.pow))
            nc.gpsimd.tensor_scalar(krn[:, :], krn[:, :], 1e12, None, ALU.min).then_inc(krn_ready, 1)
            with pool.Fori(0, NRG // 2) as it:
                for b in range(2):
                    pool.wait_ge(a_masked, it * 2 + b + 1 + FREE["a_masked"])
                    nc.gpsimd.tensor_tensor(amat[:, b, :, :], amat[:, b, :, :], eye4[:, :, :],
                                            ALU.add).then_inc(a_ready, 1)
            rsqrt_rows(2)
            rsqrt_rows(3)
            pool.wait_ge(rstd_ready, 3)
            nc.gpsimd.memset(klm[DK:DK + 2, :], 1.0).then_inc(klm_ones, 1)
            pool.wait_ge(klm_ones, 1)
            nc.gpsimd.memset(klm[DK:DK + 1, :], MSPLIT).then_inc(klm_ones, 1)
            pool.wait_ge(klm_ones, 2)
            pool.wait_ge(xn_ready, 3 * NB)
            nc.gpsimd.tensor_tensor(x[:, :, :], x[:, :, :], bo[:, :].unsqueeze(1).broadcast_to([P, NT, P]),
                                    ALU.add).then_inc(bo_added, 1)
            with pool.Fori(0, NB) as qb:
                for h in range(HEADS):
                    pool.wait_ge(qh_ready, qb * HEADS + h + 1)
                    nc.gpsimd.tensor_tensor(qhm[0:DK, h, :], qhl[0:DK, h, :], zeros16[:, :],
                                            ALU.add).then_inc(qm_copied, 1)
                with pool.Fori(0, HEADS) as h:
                    u = qb * HEADS + h
                    for j in range(1, ADDS + 1):
                        pool.wait_ge(p_ready, u * STEPS + j + 1 + FREE["p_ready"])
                        if j == 1:
                            pool.wait_ge(acc_read, u + FREE["acc_read"])
                            first = pr[:, 0, :, :]
                        else:
                            pool.wait_ge(pool_acc, u * ADDS + j - 1 + FREE["pool_acc"])
                            first = acc[:, :, :]
                        nc.gpsimd.tensor_tensor(acc[:, :, :], first, pr[:, j % 4, :, :],
                                                ALU.add).then_inc(pool_acc, 1)
            rsqrt_rows(4)
            pool.wait_ge(xn_ready, 4 * NB)
            nc.gpsimd.tensor_tensor(x[:, :, :], x[:, :, :], b2[:, :].unsqueeze(1).broadcast_to([P, NT, P]),
                                    ALU.add).then_inc(b2_added, 1)

        @block.scalar
        def _(act):
            act.sem_inc(act1_ready, FREE["act1_ready"])
            act.sem_inc(p_ready, FREE["p_ready"])
            act.sem_inc(o_saved, FREE["o_saved"])
            act.sem_inc(ff_ready, FREE["ff_ready"])
            for dst, src in loads:
                act.dma_start(dst, src).then_inc(w_in, 16)
            act.wait_ge(w_in, 16 * len(loads))
            nc.scalar.activation(ab[:, :, :], ab[:, :, :], ACT.Exp, scale=-1.0).then_inc(ab_exp, 1)

            def copy_xnT(k, b):
                act.wait_ge(xnT_psum, NB * (k - 1) + b + 1)
                nc.scalar.activation(xnT[:, BT * b:BT * (b + 1)], bank(b), ACT.Copy).then_inc(xnT_ready, 1)

            for b in range(NB):
                copy_xnT(1, b)
                for i in range(TPB * b, TPB * (b + 1)):
                    act.wait_ge(qkv_psum, i + 1)
                    nc.scalar.activation(kaq[:, i, 1, :], bank(4 + i % 4)[:, 0:P], ACT.Copy)
                    nc.scalar.activation(kv[:, i, :], bank(4 + i % 4)[:, P:3 * P], ACT.Copy).then_inc(qkv_ready, 1)
            act.wait_ge(solved, 1)
            for a in range(2):
                nc.scalar.activation(ukk[:, :, a, :].rearrange("p i (h d) -> p i h d", d=DH),
                                     ukt[:, :, :, a * DH:(a + 1) * DH], ACT.Copy).then_inc(ukk_ready, 1)
            for n in range(2 * NB):
                act.wait_ge(qo_psum, n + 1)
                dst = qT if n < NB else yT
                b = n % NB
                nc.scalar.activation(dst[:, TPB * b:TPB * (b + 1), :], bank(n).rearrange("p (t c) -> p t c", t=TPB),
                                     ACT.Copy).then_inc(qo_sbuf, 1)
            for b in range(NB):
                copy_xnT(2, b)
            act.wait_ge(shift_ready, 1)
            nc.scalar.activation(probs[:, :, :], probs[:, :, :], ACT.Exp).then_inc(gate_exp, 1)
            with act.Fori(0, EXPERTS) as e:
                for n in range(UP):
                    act.wait_ge(up_psum, e * UP + n + 1)
                    act.wait_ge(hid_ready, e * UP + n - 1 + FREE["hid_ready"])
                    nc.scalar.activation(act1[:, n % 2, :], bank(2 * (n % 2)), ACT.Silu).then_inc(act1_ready, 1)
            for b in range(NB):
                copy_xnT(3, b)
            for b in range(NB):
                act.wait_ge(kp_psum, b + 1)
                nc.scalar.activation(khh[:, BT * b:BT * (b + 1)], bank(b), ACT.Identity,
                                     bias=bk2[:, 0:1]).then_inc(kh_ready, 1)

            def save_output(u):
                act.wait_ge(pv_done, (u + 1) * STEPS + FREE["pv_done"])
                act.wait_ge(wo_ready, u + FREE["wo_ready"])
                nc.scalar.activation(osb[:, :], bank(OB), ACT.Copy).then_inc(o_saved, 1)

            def exps(u, prev, nxt):
                for j in range(STEPS):
                    act.wait_ge(st_ready, u * STEPS + j + 1)
                    act.wait_ge(pv_done, u * STEPS + j - 3 + FREE["pv_done"])
                    if j < 2:
                        act.wait_ge(pool_acc, u * ADDS - 1 + j + FREE["pool_acc"])
                    elif j < 4:
                        act.wait_ge(tail_done, u + FREE["tail_done"])
                    else:
                        act.wait_ge(pool_acc, u * ADDS + max(1, j - 4) + FREE["pool_acc"])
                    nc.scalar.activation(pr[:, j % 4, :, :], ps[:, 2 * (j % 2):2 * (j % 2) + 2, :],
                                         ACT.Exp).then_inc(p_ready, 1)
                    if j == 0 and prev:
                        save_output(u - 1)
                if not nxt:
                    save_output(u)

            with act.Fori(0, NB) as qb:
                for k in range(HEADS // 2):
                    act.wait_ge(q_psum, qb * (HEADS // 2) + k + 1)
                    for half in range(2):
                        rows = slice(DK * half, DK * (half + 1))
                        h = 2 * k + half
                        nc.scalar.activation(qhl[0:DK, h, :], ps[rows, k % 4, :], ACT.Identity,
                                             bias=bq[:, h:h + 1]).then_inc(qh_ready, 1)
                exps(qb * HEADS, False, True)
                with act.Fori(1, HEADS - 1) as h:
                    exps(qb * HEADS + h, True, True)
                exps(qb * HEADS + HEADS - 1, True, False)

            for b in range(NB):
                copy_xnT(4, b)
            with act.Fori(0, NB // 2) as it:
                for s in range(2):
                    for j in range(FF // P):
                        act.wait_ge(ff_psum, (it * 2 + s) * (FF // P) + j + 1)
                        nc.scalar.activation(ffT[:, s, j, :], bank(j), ACT.Relu,
                                             bias=b1[:, j:j + 1]).then_inc(ff_ready, 1)

        @block.vector
        def _(dve):
            V = nc.vector
            dve.sem_inc(m_ready, FREE["m_ready"])
            dve.sem_inc(a_masked, FREE["a_masked"])
            dve.sem_inc(y_ready, FREE["y_ready"])
            dve.sem_inc(hid_ready, FREE["hid_ready"])
            dve.sem_inc(down_added, FREE["down_added"])
            dve.sem_inc(tail_done, FREE["tail_done"])
            dve.sem_inc(acc_read, FREE["acc_read"])
            dve.sem_inc(mx_free, FREE["mx_free"])
            dve.sem_inc(wo_added, FREE["wo_added"])
            dve.sem_inc(fo_added, FREE["fo_added"])
            step = Steps(dve, dve_step)

            def layernorm(k):
                step(V.tensor_reduce(row_sum[:, :], x[:, :, :], AX.X, ALU.add))
                step(V.tensor_scalar(mean[:, :], row_sum[:, :], 1.0 / P, None, ALU.mult))
                step(V.tensor_tensor(xn[:, :, :], x[:, :, :], mean[:, :].unsqueeze(2).broadcast_to([P, NT, P]),
                                     ALU.subtract))
                step(V.tensor_tensor(work[:, :, :], xn[:, :, :], xn[:, :, :], ALU.mult))
                step(V.tensor_reduce(row_sum[:, :], work[:, :, :], AX.X, ALU.add))
                V.tensor_scalar(var[:, :], row_sum[:, :], 1.0 / P, EPS, ALU.mult, ALU.add).then_inc(var_ready, 1)
                dve.wait_ge(rstd_ready, k)
                for b in range(NB):
                    t = slice(TPB * b, TPB * (b + 1))
                    V.tensor_tensor(xn[:, t, :], xn[:, t, :], rstd[:, t].unsqueeze(2).broadcast_to([P, TPB, P]),
                                    ALU.mult).then_inc(xn_ready, 1)

            dve.wait_ge(x_in, 16)
            layernorm(1)
            dve.wait_ge(ab_exp, 1)
            step(V.tensor_scalar(ab[:, :, :], ab[:, :, :], 1.0, None, ALU.add))
            step(V.reciprocal(ab[:, :, :], ab[:, :, :]))
            step(V.tensor_scalar(ab[:, :, :], ab[:, :, :], 0.5, None, ALU.mult))
            V.tensor_scalar(wq[:, :], wq[:, :], DK ** -0.5, None, ALU.mult)
            step(V.tensor_scalar(bq[:, :], bq[:, :], DK ** -0.5, None, ALU.mult))
            dve.wait_ge(qkv_ready, NT)
            raw_k = kv[:, :, 0:P]
            step(V.tensor_tensor(work[:, :, :], raw_k, raw_k, ALU.mult))
            V.tensor_reduce(kss[:, :], work[:, :, :].rearrange("p i (h d) -> p (i h) d", d=DH), AX.X,
                            ALU.add).then_inc(kss_ready, 1)
            heads = lambda ap: ap.rearrange("p i (h d) -> p i h d", d=DH)
            per_head = lambda ap: ap.unsqueeze(1).unsqueeze(3).broadcast_to([P, NT, HEADS, DH])
            V.tensor_tensor(ukt[:, :, :, 0:DH], heads(kv[:, :, P:2 * P]), per_head(ab[:, 1, :]), ALU.mult)
            dve.wait_ge(krn_ready, 1)
            step(V.tensor_tensor(heads(kn), heads(raw_k),
                                 krn[:, :].rearrange("p (i h) -> p i h", h=HEADS).unsqueeze(3)
                                 .broadcast_to([P, NT, HEADS, DH]), ALU.mult))
            step(V.tensor_tensor(heads(kaq[:, :, 0, :]), heads(kn), per_head(ab[:, 0, :]), ALU.mult))
            step(V.tensor_copy(ukt[:, :, :, DH:2 * DH], heads(kaq[:, :, 0, :])))

            def weighted_sum(i, which):
                n = i * HEADS
                row = kaq[:, i, which, :].unsqueeze(1).broadcast_to([P, i, P])
                step(V.tensor_tensor(prod1[:, 0:i, :], row, ukk[:, 0:i, 2, :], ALU.mult))
                step(V.tensor_reduce(dots[:, 0:n], prod1[:, 0:i, :].rearrange("p s (h d) -> p (s h) d", d=DH), AX.X,
                                     ALU.add))
                step(V.tensor_tensor(prod2[:, 0:i, :].rearrange("p s (h c) -> p (s h) c", h=HEADS),
                                     ukt[:, 0:i, :, :].rearrange("p s h c -> p (s h) c"),
                                     dots[:, 0:n].unsqueeze(2).broadcast_to([P, n, 2 * DH]), ALU.mult))
                step(V.tensor_reduce(corr[:, :], prod2[:, 0:i, :].rearrange("p s c -> p c s"), AX.X, ALU.add))

            for i in range(1, SUB):
                weighted_sum(i, 0)
                done = V.tensor_tensor(ukt[:, i, :, :].rearrange("p h c -> p (h c)"),
                                       ukt[:, i, :, :].rearrange("p h c -> p (h c)"), corr[:, :], ALU.subtract)
                if i < SUB - 1:
                    step(done)
            done.then_inc(solved, 1)
            dve.wait_ge(solved, 1)
            step(V.memset(kaq[:, 0, 0, :], 0.0))
            corr_v = corr[:, :].rearrange("p (h two d) -> p two h d", two=2, h=HEADS)
            for i in range(1, SUB):
                weighted_sum(i, 1)
                V.tensor_copy(kaq[:, i, 0, :].rearrange("p (h d) -> p h d", d=DH), corr_v[:, 0])
                qrow = kaq[:, i, 1, :].rearrange("p (h d) -> p h d", d=DH)
                done = V.tensor_tensor(qrow, qrow, corr_v[:, 1], ALU.subtract)
                if i < SUB - 1:
                    step(done)
            done.then_inc(qo_ready, 1)
            V.memset(mst[:, 0, :], 0.0).then_inc(m_ready, 1)

            def mask_transitions(c, b):
                dve.wait_ge(a_psum, c + 1)
                V.tensor_tensor(amat[:, b, :, :], ps[:, b, :].rearrange("p (g c) -> p g c", g=RG), negmask[:, :, :],
                                ALU.mult).then_inc(a_masked, 1)

            def states(c, b):
                for g in range(RG):
                    n = c * RG + g
                    dve.wait_ge(m_psum, n + 1 + FREE["m_psum"])
                    V.tensor_tensor(mst[:, (g + 1) % RG, :], ps[:, 2 + b, g * P:(g + 1) * P], mask[:, :],
                                    ALU.mult).then_inc(m_ready, 1)
                dve.wait_ge(y_psum, c + 1)
                cols = yT[:, :, bass.ds(c * RG, RG)].rearrange("p i g -> p g i")
                V.tensor_tensor(cols, ps[:, 4 + b, 0:RG * SUB].rearrange("p (g i) -> p g i", g=RG), cols,
                                ALU.add).then_inc(y_ready, 1)

            dve.wait_ge(qo_sbuf, 2 * NB)
            mask_transitions(0, 0)
            with dve.Fori(0, NRG // 2 - 1) as it:
                for b in range(2):
                    mask_transitions(it * 2 + b + 1, 1 - b)
                    states(it * 2 + b, b)
            mask_transitions(NRG - 1, 1)
            states(NRG - 2, 0)
            states(NRG - 1, 1)
            for b in range(NB):
                dve.wait_ge(proj_psum, b + 1)
                t = slice(TPB * b, TPB * (b + 1))
                V.tensor_tensor(x[:, t, :], ps[:, 4 + b, :].rearrange("p (t c) -> p t c", t=TPB), x[:, t, :],
                                ALU.add).then_inc(x_added, 1)
            dve.wait_ge(x_added, NB)
            layernorm(2)

            dve.wait_ge(gate_psum, 1)
            logits = ps[:, 4, 0:P].rearrange("p (t e) -> p t e", e=EXPERTS)
            over_e = lambda ap: ap.unsqueeze(2).broadcast_to([P, NT, EXPERTS])
            step(V.tensor_reduce(r1[:, :], logits, AX.X, ALU.max))
            V.tensor_tensor(probs[:, :, :], logits, over_e(r1[:, :]), ALU.subtract).then_inc(shift_ready, 1)
            dve.wait_ge(gate_exp, 1)
            step(V.tensor_reduce(r1[:, :], probs[:, :, :], AX.X, ALU.add))
            step(V.reciprocal(r1[:, :], r1[:, :]))
            step(V.tensor_tensor(probs[:, :, :], probs[:, :, :], over_e(r1[:, :]), ALU.mult))
            other = probs[:, :, :].unsqueeze(2).broadcast_to([P, NT, EXPERTS, EXPERTS])
            own = probs[:, :, :].unsqueeze(3).broadcast_to([P, NT, EXPERTS, EXPERTS])
            V.tensor_tensor(cmp_gt[:, :, :, :], other, own, ALU.is_gt)
            step(V.tensor_tensor(cmp_eq[:, :, :, :], other, own, ALU.is_equal))
            step(V.tensor_tensor(cmp_eq[:, :, :, :], cmp_eq[:, :, :, :],
                                 earlier[:, :, :].unsqueeze(1).broadcast_to([P, NT, EXPERTS, EXPERTS]), ALU.mult))
            step(V.tensor_tensor(cmp_gt[:, :, :, :], cmp_gt[:, :, :, :], cmp_eq[:, :, :, :], ALU.add))
            step(V.tensor_reduce(rank[:, :, :], cmp_gt[:, :, :, :], AX.X, ALU.add))
            step(V.scalar_tensor_tensor(gatew[:, :, :], rank[:, :, :], float(TOPK), probs[:, :, :], ALU.is_lt,
                                        ALU.mult))

            def add_expert(e, b):
                n = e * NB + b
                dve.wait_ge(down_psum, n + 1)
                dve.wait_ge(down_added, n + FREE["down_added"])
                for t in range(TPB):
                    i = TPB * b + t
                    last = V.scalar_tensor_tensor(x[:, i, :], ps[:, 4 + b % 2, t * P:(t + 1) * P],
                                                  gatew[:, i, bass.ds(e, 1)], x[:, i, :], ALU.mult, ALU.add)
                last.then_inc(down_added, 1)

            with dve.Fori(0, EXPERTS) as e:
                for n in range(UP):
                    dve.wait_ge(gt_psum, e * UP + n + 1)
                    dve.wait_ge(act1_ready, e * UP + n + 1 + FREE["act1_ready"])
                    V.tensor_tensor(hidT[:, (n // 2) % 2, n % 2, :], ps[:, 2 * (n % 2) + 1, :], act1[:, n % 2, :],
                                    ALU.mult).then_inc(hid_ready, 1)
                    if n % 2 == 0 and n > 0:
                        add_expert(e, n // 2 - 1)
                add_expert(e, NB - 1)
            dve.wait_ge(down_added, EXPERTS * NB + FREE["down_added"])
            layernorm(3)

            for b in range(NB):
                dve.wait_ge(kh_ready, b + 1)
                cols = slice(BT * b, BT * (b + 1))
                V.scalar_tensor_tensor(klm[0:DK, cols], ps[0:DK, b, :], bk2[0:DK, 0:1], khh[0:DK, cols], ALU.add,
                                       ALU.subtract).then_inc(kl_ready, 1)
            for n in range(2):
                dve.wait_ge(vp_psum, n + 1)
                V.tensor_tensor(vt[:, 8 * n:8 * (n + 1), :], ps[:, 4 + n, :].rearrange("p (t d) -> p t d", d=DK),
                                bv[:, :].unsqueeze(1).broadcast_to([P, 8, DK]), ALU.add).then_inc(v_ready, 1)

            def chunk_max(u, m):
                dve.wait_ge(mx_ready, u * NCH + m + 1)
                V.tensor_reduce(cmax[:, m // NB, m % NB:m % NB + 1], bank(MX + m % 2), AX.X,
                                ALU.max).then_inc(mx_free, 1)

            def split_max(u):
                dve.wait_ge(mx_free, (u + 1) * NCH + FREE["mx_free"])
                V.tensor_reduce(nmax[:, :], cmax[:, :, :], AX.X, ALU.max, negate=True).then_inc(max_step, 1)
                dve.wait_ge(max_step, u * 2 + 1)
                V.tensor_scalar(m16[:, :, 0], nmax[:, :], 1.0 / MSPLIT, None, ALU.mult).then_inc(max_step, 1)
                dve.wait_ge(max_step, u * 2 + 2)
                V.scalar_tensor_tensor(m16[:, :, 1], m16[:, :, 0], -MSPLIT, nmax[:, :], ALU.mult,
                                       ALU.add).then_inc(rowmax_ready, 1)

            def place_max(u, h):
                dve.wait_ge(tr_ready, u + 1)
                V.tensor_copy(qhm[DK:DK + 2, bass.ds(h, 1), :].rearrange("p o c -> p (o c)"),
                              small16[DK:DK + 2, 0:BT]).then_inc(t2_ready, 1)

            def finish_sum(u):
                dve.wait_ge(p_ready, (u + 1) * STEPS + FREE["p_ready"])
                V.tensor_tensor(tail[:, :, :], pr[:, 2, :, :], pr[:, 3, :, :], ALU.add).then_inc(tail_done, 1)
                dve.wait_ge(tail_done, u + 1 + FREE["tail_done"])
                dve.wait_ge(pool_acc, (u + 1) * ADDS + FREE["pool_acc"])
                V.tensor_tensor(tail[:, :, :], tail[:, :, :], acc[:, :, :], ALU.add).then_inc(acc_read, 1)
                dve.wait_ge(acc_read, u + 1 + FREE["acc_read"])
                V.tensor_tensor(keysum[:, :], tail[:, 0, :], tail[:, 1, :], ALU.add).then_inc(keysum_ready, 1)

            def read_denominator(u):
                dve.wait_ge(den_ready, u + 1)
                V.reciprocal(rden[:, :], ps[:, SM, 0:TPB]).then_inc(den_read, 1)

            def add_head(u, qb):
                dve.wait_ge(wo_ready, u + 1 + FREE["wo_ready"])
                dve.wait_ge(wo_added, u + FREE["wo_added"])
                dve.wait_ge(den_read, u + 1)
                for t in range(TPB):
                    row = x[:, bass.ds(qb * TPB + t, 1), :].rearrange("p o c -> p (o c)")
                    last = V.scalar_tensor_tensor(row, ps[:, SM, t * P:(t + 1) * P], rden[:, t:t + 1], row, ALU.mult,
                                                  ALU.add)
                last.then_inc(wo_added, 1)

            def head(u, qb, h, prev, nxt):
                m = 0
                for j in range(STEPS):
                    if j == 0 and prev:
                        finish_sum(u - 1)
                    if nxt:
                        for _ in range(MAX_CHUNKS[j]):
                            chunk_max(u + 1, m)
                            m += 1
                    if j == 2 and prev:
                        read_denominator(u - 1)
                    if j == 3 and prev:
                        add_head(u - 1, qb)
                    if j == 6 and nxt:
                        split_max(u + 1)
                    if j == 7 and nxt:
                        place_max(u + 1, h + 1)
                if not nxt:
                    finish_sum(u)
                    read_denominator(u)
                    add_head(u, qb)

            dve.wait_ge(bo_added, 1)
            with dve.Fori(0, NB) as qb:
                for k in range(HEADS // 2):
                    dve.wait_ge(qh_ready, qb * HEADS + 2 * k + 2)
                    for half in range(2):
                        rows = slice(DK * half, DK * (half + 1))
                        h = 2 * k + half
                        V.scalar_tensor_tensor(qhl[DK:2 * DK, h, :], ps[rows, k % 4, :], bq[:, h:h + 1],
                                               qhl[0:DK, h, :], ALU.add, ALU.subtract).then_inc(ql_ready, 1)
                u0 = qb * HEADS
                for m in range(NCH):
                    chunk_max(u0, m)
                split_max(u0)
                place_max(u0, 0)
                head(u0, qb, 0, False, True)
                with dve.Fori(1, HEADS - 1) as h:
                    head(u0 + h, qb, h, True, True)
                head(u0 + HEADS - 1, qb, HEADS - 1, True, False)

            dve.wait_ge(wo_added, NB * HEADS + FREE["wo_added"])
            layernorm(4)
            dve.wait_ge(b2_added, 1)
            with dve.Fori(0, NB // 2) as it:
                for s in range(2):
                    dve.wait_ge(fo_psum, it * 2 + s + 1)
                    t = bass.ds((it * 2 + s) * TPB, TPB)
                    V.tensor_tensor(x[:, t, :], ps[:, 4 + s, :].rearrange("p (t c) -> p t c", t=TPB), x[:, t, :],
                                    ALU.add).then_inc(fo_added, 1)

        @block.tensor
        def _(pe):
            mm = nc.tensor.matmul
            pe.sem_inc(m_psum, FREE["m_psum"])
            pe.sem_inc(pv_done, FREE["pv_done"])
            pe.sem_inc(wo_ready, FREE["wo_ready"])

            def transpose_xn(k, b):
                pe.wait_ge(xn_ready, NB * (k - 1) + b + 1)
                for t in range(TPB):
                    last = nc.tensor.transpose(ps[:, b, t * P:(t + 1) * P], xn[:, TPB * b + t, :], ident[:, :])
                last.then_inc(xnT_psum, 1)

            def tile(i):
                return xnT[:, i * P:(i + 1) * P]

            pe.wait_ge(consts, 1)
            pe.wait_ge(w_in, 16 * len(loads))
            for b in range(NB):
                transpose_xn(1, b)
            for b in range(NB):
                pe.wait_ge(xnT_ready, b + 1)
                for i in range(TPB * b, TPB * (b + 1)):
                    if i >= 4:
                        pe.wait_ge(qkv_ready, i - 3)
                    mm(ps[:, 4 + i % 4, 0:3 * P], tile(i), wqkv[:, :], start=True, stop=True).then_inc(qkv_psum, 1)
            pe.wait_ge(qo_ready, 1)
            for n in range(2 * NB):
                which = 1 if n < NB else 0
                for t in range(TPB):
                    i = TPB * (n % NB) + t
                    last = nc.tensor.transpose(ps[:, n, t * P:(t + 1) * P], kaq[:, i, which, :], ident[:, :])
                last.then_inc(qo_psum, 1)
            pe.wait_ge(qo_sbuf, 2 * NB)

            def prepare(c, b, turn):
                pe.wait_ge(sub_in[b], (turn + 1) * 16)
                pe.wait_ge(a_masked, c - 1 + FREE["a_masked"])
                part = lambda g, k: sub[:, b, g, k * P:(k + 1) * P]
                for g in range(RG):
                    last = mm(ps[:, b % 2, g * P:(g + 1) * P], part(g, 1), part(g, 2),
                              start=True, stop=True)
                last.then_inc(a_psum, 1)
                pe.wait_ge(m_ready, (c - 1) * RG + 1 + FREE["m_ready"])
                for g in range(RG):
                    mm(ps[:, 2 + b % 2, g * P:(g + 1) * P], part(g, 2), part(g, 0), start=(g == 0),
                       stop=False, skip_group_check=True)

            def advance(c, b):
                pe.wait_ge(a_ready, c + 1)
                pe.wait_ge(y_ready, c - 1 + FREE["y_ready"])
                for g in range(RG):
                    pe.wait_ge(m_ready, c * RG + g + 1 + FREE["m_ready"])
                    mm(ps[:, 2 + b % 2, g * P:(g + 1) * P], amat[:, b % 2, g, :], mst[:, g, :], start=False,
                       stop=True, skip_group_check=True).then_inc(m_psum, 1)
                    last = mm(ps[:, 4 + b % 2, g * SUB:(g + 1) * SUB], mst[:, g, :],
                              qT[:, :, bass.ds(c * RG + g, 1)].rearrange("p i o -> p (i o)"), start=True, stop=True)
                last.then_inc(y_psum, 1)

            prepare(0, 0, 0)
            with pe.Fori(0, NRG // SLOTS - 1) as it:
                for b in range(SLOTS):
                    prepare(it * SLOTS + b + 1, (b + 1) % SLOTS, it + (b + 1) // SLOTS)
                    advance(it * SLOTS + b, b)
            for b in range(SLOTS):
                if b < SLOTS - 1:
                    prepare(NRG - SLOTS + b + 1, b + 1, NRG // SLOTS - 1)
                advance(NRG - SLOTS + b, b)
            pe.wait_ge(y_ready, NRG + FREE["y_ready"])
            for b in range(NB):
                for t in range(TPB):
                    last = mm(ps[:, 4 + b, t * P:(t + 1) * P], yT[:, TPB * b + t, :], wproj[:, :], start=True, stop=True)
                last.then_inc(proj_psum, 1)

            for b in range(NB):
                transpose_xn(2, b)
            pe.wait_ge(xnT_ready, 2 * NB)
            for i in range(NT):
                last = mm(ps[:, 4, i * EXPERTS:(i + 1) * EXPERTS], tile(i), gate[:, :], start=True, stop=True)
            last.then_inc(gate_psum, 1)

            def expert_down(e, b, s):
                n = e * NB + b
                pe.wait_ge(hid_ready, n * 2 + 2 + FREE["hid_ready"])
                pe.wait_ge(down_added, n - 1 + FREE["down_added"])
                for t in range(TPB):
                    for j in range(HID // P):
                        last = mm(ps[:, 4 + b % 2, t * P:(t + 1) * P], hidT[:, b % 2, j, t * P:(t + 1) * P],
                                  ew2[:, s, j, :], start=(j == 0), stop=(j == HID // P - 1))
                last.then_inc(down_psum, 1)

            with pe.Fori(0, EXPERTS // 2) as ep:
                for s in range(2):
                    e = ep * 2 + s
                    pe.wait_ge(ew_in[s], ep * 48 + 48)
                    for n in range(UP):
                        b, j = n // 2, n % 2
                        src = xnT[:, BT * b:BT * (b + 1)]
                        pe.wait_ge(act1_ready, e * UP + n - 1 + FREE["act1_ready"])
                        mm(bank(2 * j), ew1[:, s, j * P:(j + 1) * P], src, start=True, stop=True).then_inc(up_psum, 1)
                        pe.wait_ge(hid_ready, e * UP + n - 1 + FREE["hid_ready"])
                        mm(bank(2 * j + 1), ew3[:, s, j * P:(j + 1) * P], src, start=True,
                           stop=True).then_inc(gt_psum, 1)
                        if j == 0 and n > 0:
                            expert_down(e, b - 1, s)
                    expert_down(e, NB - 1, s)

            for b in range(NB):
                transpose_xn(3, b)
            for b in range(NB):
                pe.wait_ge(xnT_ready, 2 * NB + b + 1)
                mm(bank(b), wk2[:, :, :].rearrange("p a d -> p (a d)"), xnT[:, BT * b:BT * (b + 1)], start=True,
                   stop=True).then_inc(kp_psum, 1)
            for n in range(2):
                for t in range(8):
                    last = mm(ps[:, 4 + n, t * DK:(t + 1) * DK], tile(8 * n + t), wv[:, :], start=True, stop=True)
                last.then_inc(vp_psum, 1)
            pe.wait_ge(kl_ready, NB)
            pe.wait_ge(v_ready, 2)
            pe.wait_ge(klm_ones, 2)

            def scores(u, h, j):
                pe.wait_ge(p_ready, u * STEPS + j - 1 + FREE["p_ready"])
                for a in range(2):
                    keys = slice((2 * j + a) * P, (2 * j + a + 1) * P)
                    dst = bank(2 * (j % 2) + a)
                    mm(dst, khh[:, keys], qhl[:, bass.ds(h, 1), :].rearrange("p o c -> p (o c)"), start=True, stop=False)
                    last = mm(dst, klm[:, keys], qhm[:, bass.ds(h, 1), :].rearrange("p o c -> p (o c)"), start=False,
                              stop=True)
                last.then_inc(st_ready, 1)

            def max_scores(u, h, m):
                pe.wait_ge(mx_free, u * NCH + m - 1 + FREE["mx_free"])
                qt, kb = m // NB, m % NB
                mm(bank(MX + m % 2), qhl[:, bass.ds(h, 1), qt * P:(qt + 1) * P].rearrange("p o c -> p (o c)"),
                   khh[:, kb * BT:(kb + 1) * BT], start=True, stop=True).then_inc(mx_ready, 1)

            def turn_max(u):
                pe.wait_ge(rowmax_ready, u + 1)
                pe.wait_ge(wo_added, u - 1 + FREE["wo_added"])
                for qt in range(TPB):
                    last = nc.tensor.transpose(small16[DK:DK + 2, qt * P:(qt + 1) * P], m16[:, qt, :], ident16[:, :])
                last.then_inc(tr_ready, 1)

            def weigh_values(u, j):
                pe.wait_ge(p_ready, u * STEPS + j + 1 + FREE["p_ready"])
                if j == 0:
                    pe.wait_ge(o_saved, u + FREE["o_saved"])
                for a in range(2):
                    last = mm(ps[DK * a:DK * (a + 1), OB, :], vt[:, 2 * j + a, :], pr[:, j % 4, a, :], start=(j == 0),
                              stop=(j == STEPS - 1))
                last.then_inc(pv_done, 1)

            def denominator(u):
                pe.wait_ge(keysum_ready, u + 1)
                for t in range(TPB):
                    last = mm(ps[:, SM, t:t + 1], keysum[:, t * P:(t + 1) * P], ones[:, :], start=True, stop=True)
                last.then_inc(den_ready, 1)

            def project_head(u, h):
                pe.wait_ge(den_read, u + 1)
                pe.wait_ge(o_saved, u + 1 + FREE["o_saved"])
                for t in range(TPB):
                    last = mm(ps[:, SM, t * P:(t + 1) * P], osb[:, t * P:(t + 1) * P],
                              wo2[:, bass.ds(h, 1), :].rearrange("p o c -> p (o c)"), start=True, stop=True)
                last.then_inc(wo_ready, 1)

            def head(u, h, prev, nxt):
                m = 0
                for j in range(STEPS):
                    if j == 0:
                        pe.wait_ge(t2_ready, u + 1)
                    scores(u, h, j)
                    if nxt:
                        for _ in range(MAX_CHUNKS[j]):
                            max_scores(u + 1, h + 1, m)
                            m += 1
                    if j == 7 and nxt:
                        turn_max(u + 1)
                    if j == 2 and prev:
                        denominator(u - 1)
                    if j == 3 and prev:
                        project_head(u - 1, h - 1)
                    if j > 0:
                        weigh_values(u, j - 1)
                    elif prev:
                        weigh_values(u - 1, STEPS - 1)
                if not nxt:
                    weigh_values(u, STEPS - 1)
                    denominator(u)
                    project_head(u, h)

            with pe.Fori(0, NB) as qb:
                u0 = qb * HEADS
                for k in range(HEADS // 2):
                    if k < 4:
                        pe.wait_ge(p_ready, u0 * STEPS + FREE["p_ready"])
                    else:
                        pe.wait_ge(ql_ready, qb * HEADS + 2 * (k - 3))
                    mm(bank(k % 4), wq[:, k * P:(k + 1) * P], xnT[:, bass.ds(qb * BT, BT)], start=True,
                       stop=True).then_inc(q_psum, 1)
                pe.wait_ge(ql_ready, qb * HEADS + HEADS)
                pe.wait_ge(qm_copied, qb * HEADS + HEADS)
                for m in range(NCH):
                    max_scores(u0, 0, m)
                turn_max(u0)
                head(u0, 0, False, True)
                with pe.Fori(1, HEADS - 1) as h:
                    head(u0 + h, h, True, True)
                head(u0 + HEADS - 1, HEADS - 1, True, False)

            for b in range(NB):
                transpose_xn(4, b)
            NF = FF // P
            pe.wait_ge(xnT_ready, 4 * NB)
            with pe.Fori(0, NB // 2) as it:
                for s in range(2):
                    n = it * 2 + s
                    for j in range(NF):
                        pe.wait_ge(ff_ready, n * NF + j - 3 + FREE["ff_ready"])
                        mm(bank(j), w1[:, j * P:(j + 1) * P], xnT[:, bass.ds(n * BT, BT)], start=True,
                           stop=True).then_inc(ff_psum, 1)
                    pe.wait_ge(ff_ready, n * NF + NF + FREE["ff_ready"])
                    pe.wait_ge(fo_added, n - 1 + FREE["fo_added"])
                    for t in range(TPB):
                        for j in range(NF):
                            last = mm(ps[:, 4 + s, t * P:(t + 1) * P], ffT[:, s, j, t * P:(t + 1) * P], w2[:, j, :],
                                      start=(j == 0), stop=(j == NF - 1))
                    last.then_inc(fo_psum, 1)


def kernel(**inputs):
    import numpy as np
    import concourse.bacc as bacc
    from concourse.bass_utils import run_bass_kernel_spmd

    g = {name: np.asarray(a) for name, a in inputs.items()}
    arrays = {
        "x": g["L0_attn_x"],
        "wqkv": np.concatenate([g["L0_attn_Wq"].T, g["L0_attn_Wk"].T, g["L0_attn_Wv"].T], axis=1),
        "wproj": g["L0_attn_Wproj"].T,
        "alpha": g["L0_attn_alpha_raw"], "beta": g["L0_attn_beta_raw"],
        "gate": g["L0_ffn_gate_w"].T, "ew1": g["L0_ffn_w1"], "ew2": g["L0_ffn_w2"], "ew3": g["L0_ffn_w3"],
        "wq": g["L1_attn_Wq"], "bq": g["L1_attn_bq"].reshape(HEADS, DK).T,
        "wk": g["L1_attn_Wk"], "bk": g["L1_attn_bk"].reshape(DK, 1),
        "wv": g["L1_attn_Wv"], "bv": g["L1_attn_bv"], "wo": g["L1_attn_Wo"], "bo": g["L1_attn_bo"],
        "w1": g["L1_ffn_W1"], "b1": g["L1_ffn_b1"].reshape(FF // P, P).T,
        "w2": g["L1_ffn_W2"], "b2": g["L1_ffn_b2"],
    }
    arrays = {name: np.ascontiguousarray(a) for name, a in arrays.items()}
    nc = bacc.Bacc("TRN2", target_bir_lowering=False, num_devices=1)
    io = {name: nc.dram_tensor("in_" + name, a.shape, mybir.dt.from_np(a.dtype), kind="ExternalInput").ap()
          for name, a in arrays.items()}
    shape = arrays["x"].shape
    out = nc.dram_tensor("out", shape, F32, kind="ExternalOutput").ap()
    build(nc, io, out)
    result = run_bass_kernel_spmd(nc, [{"in_" + name: a for name, a in arrays.items()}], core_ids=[0])
    return result.results[0]["out"]
```

```python
from contextlib import ExitStack

import concourse.bass as bass
from concourse import mybir

ALU = mybir.AluOpType
ACT = mybir.ActivationFunctionType
AX = mybir.AxisListType
F32 = mybir.dt.float32
F16 = mybir.dt.float16

P = 128
T = 2048
NT = T // P
NB = 4
BT = T // NB
TPB = NT // NB
HEADS = 16
DH = P // HEADS
SUB = NT
NSUB = T // SUB
RG = 4
NRG = NSUB // RG
SLOTS = 4
EXPERTS, HID, TOPK = 8, 256, 2
DK = 64
FF = 512
KT = T // P
QPIECE = 8
STEPS = KT // 2
MSPLIT = 64.0
EPS = 1e-5
MAX_CHUNKS = [2, 2, 3, 3, 3, 3, 0, 0]


FREE = {"y_ready": 2, "act1_ready": 2, "hid_ready": 2, "down_added": 3, "p_ready": 2, "pv_done": 4,
          "pool_acc": 7, "keysum_ready": 1, "mx_free": 2, "o_saved": 1, "wo_ready": 1, "wo_added": 1,
          "ff_ready": 4, "fo_added": 2, "m_psum": 16}


class Steps:

    def __init__(self, engine, sem):
        self.engine, self.sem, self.count = engine, sem, 0

    def __call__(self, instruction):
        instruction.then_inc(self.sem, 1)
        self.count = self.count + 1
        self.engine.wait_ge(self.sem, self.count)


def build(nc, io, out):
    with ExitStack() as ctx:
        def sb(name, shape, dt=F32, scope=ctx):
            return scope.enter_context(nc.sbuf_tensor(name, shape, dt))

        def sem(name):
            return ctx.enter_context(nc.semaphore(name))

        x = sb("x", [P, NT, P])
        xn = sb("xn", [P, NT, P])
        xnT = sb("xnT", [P, T])
        work = sb("work", [P, NT, P])
        row_sum = sb("row_sum", [P, NT])
        mean = sb("mean", [P, NT])
        var = sb("var", [P, NT])
        rstd = sb("rstd", [P, NT])
        ident = sb("ident", [P, P])
        neg_ident = sb("neg_ident", [P, P])
        ident16 = sb("ident16", [P, P], F16)
        mask = sb("mask", [P, P])
        negmask = sb("negmask", [P, RG, P])
        eye4 = sb("eye4", [P, RG, P])
        ones = sb("ones", [P, 1])
        zeros16 = sb("zeros16", [DK, BT], F16)
        minus_half = sb("minus_half", [P, 2 * P])
        earlier = sb("earlier", [P, EXPERTS, EXPERTS])
        wqkv = sb("wqkv", [P, 3 * P])
        wproj = sb("wproj", [P, P])
        ab = sb("ab", [P, 2, HEADS])
        gate = sb("gate", [P, EXPERTS])
        wq = sb("wq", [P, HEADS * DK])
        bq = sb("bq", [DK, HEADS])
        wk2 = sb("wk2", [P, 2, DK])
        bk2 = sb("bk2", [P, 1])
        wv = sb("wv", [P, DK])
        bv = sb("bv", [P, DK])
        wo2 = sb("wo2", [P, HEADS, P])
        bo = sb("bo", [P, P])
        w1 = sb("w1", [P, FF])
        b1 = sb("b1", [P, FF // P])
        w2 = sb("w2", [P, FF // P, P])
        b2 = sb("b2", [P, P])

        a_scope = ExitStack()
        sa_ = lambda name, shape, dt=F32: sb(name, shape, dt, a_scope)
        kaq = sa_("kaq", [P, NT, 2, P])
        kv = sa_("kv", [P, NT, 2 * P])
        ukk = sa_("ukk", [P, NT, 3, P])
        dots = sa_("dots", [P, NT * HEADS])
        corr = sa_("corr", [P, 2 * P])
        qdots = sa_("qdots", [P, 2, NT * HEADS])
        qprod = sa_("qprod", [P, 2, QPIECE, 2, P])
        kss = sa_("kss", [P, NT * HEADS])
        krn = sa_("krn", [P, NT * HEADS])
        sub = sa_("sub", [P, SLOTS, RG, 3 * P])
        amat = sa_("amat", [P, SLOTS, RG, P])
        mst = sa_("mst", [P, RG, P])
        qT = sa_("qT", [P, NT, P])
        yT = sa_("yT", [P, NT, P])
        kn = ukk[:, :, 2, :]
        prod1 = work
        prod2 = kv
        qk = [xn[:, :, :], xnT[:, :].rearrange("p (i c) -> p i c", c=P)]
        a_scope.close()

        sbb = sb
        ew1 = sbb("ew1", [P, 2, HID])
        ew3 = sbb("ew3", [P, 2, HID])
        ew2 = sbb("ew2", [P, 2, HID // P, P])
        act1 = sbb("act1", [P, 2, BT])
        hidT = sbb("hidT", [P, 2, HID // P, BT])
        r1 = sbb("r1", [P, NT])
        probs = sbb("probs", [P, NT, EXPERTS])
        cmp_gt = sbb("cmp_gt", [P, NT, EXPERTS, EXPERTS])
        cmp_eq = sbb("cmp_eq", [P, NT, EXPERTS, EXPERTS])
        rank = sbb("rank", [P, NT, EXPERTS])
        gatew = sbb("gatew", [P, NT, EXPERTS])
        khh = sb("khh", [P, T], F16)
        klm = sb("klm", [DK + 2, T], F16)
        vt = sb("vt", [P, KT, DK])
        qhl = sb("qhl", [P, HEADS, BT], F16)
        qhm = sb("qhm", [DK + 2, HEADS, BT], F16)
        pr = sb("pr", [P, 4, 2, BT])
        acc = sb("acc", [P, 2, BT])
        keysum = sb("keysum", [P, BT])
        osb = sb("osb", [P, BT])
        cmax = sb("cmax", [P, TPB, NB])
        nmax = sb("nmax", [P, TPB])
        m16 = sb("m16", [P, TPB, 2], F16)
        rden = sb("rden", [P, TPB])
        ffT = sb("ffT", [P, 2, FF // P, BT])

        ps = ctx.enter_context(nc.psum_tensor("ps", [P, 8, BT], F32))

        def bank(b):
            return ps[:, b, :]

        MX, OB, SM = 4, 6, 7
        small16 = ps[:, SM, :].bitcast(F16)

        scratch = nc.dram_tensor("scratch", [T, 3 * P], F32, kind="Internal").ap()

        (x_in, w_in, consts, pool_step, dve_step, xn_ready, xnT_psum, xnT_ready, var_ready, rstd_ready,
         ab_exp, qkv_psum, qkv_ready, kss_ready, krn_ready, kn_ready, solved, scratch_out, qk_ready, qdots_ready,
         qprod_ready, qprod_used, qo_psum, qo_sbuf, a_psum, a_masked, a_ready, m_psum, m_ready, y_psum, y_ready, proj_psum, x_added,
         gate_psum, shift_ready, gate_exp, up_psum, gt_psum, act1_ready, hid_ready, down_psum, down_added,
         kp_psum, kh_ready, kl_ready, vp_psum, v_ready, bo_added, q_psum, qh_ready, ql_ready, qm_copied,
         st_ready, p_ready, pv_done, pool_acc, keysum_ready, mx_ready, mx_free,
         max_step, rowmax_ready, tr_ready, t2_ready, o_saved, den_ready, den_read, wo_ready, wo_added,
         b2_added, ff_psum, ff_ready, fo_psum, fo_added, y_out, klm_ones) = (sem(n) for n in """
            x_in w_in consts pool_step dve_step xn_ready xnT_psum xnT_ready var_ready rstd_ready ab_exp
            qkv_psum qkv_ready kss_ready krn_ready kn_ready solved scratch_out qk_ready qdots_ready qprod_ready qprod_used qo_psum qo_sbuf a_psum
            a_masked a_ready m_psum m_ready y_psum y_ready proj_psum x_added gate_psum shift_ready gate_exp
            up_psum gt_psum act1_ready hid_ready down_psum down_added kp_psum kh_ready kl_ready vp_psum v_ready
            bo_added q_psum qh_ready ql_ready qm_copied st_ready p_ready pv_done pool_acc
            keysum_ready mx_ready mx_free max_step rowmax_ready tr_ready t2_ready o_saved den_ready den_read
            wo_ready wo_added b2_added ff_psum ff_ready fo_psum fo_added y_out klm_ones""".split())
        sub_in = [sem(f"sub_in{b}") for b in range(SLOTS)]
        ew_in = [sem(f"ew_in{b}") for b in range(2)]
        block = ctx.enter_context(nc.Block())

        xv = io["x"].rearrange("o (p i) c -> (o p) i c", p=P)
        ov = out.rearrange("o (p i) c -> (o p) i c", p=P)
        loads = [(wqkv[:, :], io["wqkv"]), (ab[:, 0, :], io["alpha"].partition_broadcast(P)),
                 (ab[:, 1, :], io["beta"].partition_broadcast(P)),
                 (wproj[:, :], io["wproj"]), (gate[:, :], io["gate"]), (wq[:, :], io["wq"]),
                 (bq[:, :], io["bq"]), (wk2[:, 0, :], io["wk"]), (wk2[:, 1, :], io["wk"]),
                 (bk2[0:DK, :], io["bk"]), (bk2[DK:2 * DK, :], io["bk"]), (wv[:, :], io["wv"]),
                 (bv[:, :], io["bv"].partition_broadcast(P)),
                 (wo2[0:DK, :, :], io["wo"].rearrange("(h d) m -> d h m", h=HEADS)),
                 (wo2[DK:2 * DK, :, :], io["wo"].rearrange("(h d) m -> d h m", h=HEADS)),
                 (bo[:, :], io["bo"].partition_broadcast(P)),
                 (w1[:, :], io["w1"]), (b1[:, :], io["b1"]),
                 (w2[:, :, :], io["w2"].rearrange("(j p) m -> p j m", p=P)),
                 (b2[:, :], io["b2"].partition_broadcast(P))]
        UP = 2 * NB
        NCH = TPB * NB
        ADDS = STEPS - 1

        def pieces(i):
            n = 1 + sum(-(-j // QPIECE) for j in range(1, i))
            return [(n + k, s, min(s + QPIECE, i)) for k, s in enumerate(range(0, i, QPIECE))]

        @block.sync
        def _(sp):
            sp.dma_start(x[:, :, :], xv).then_inc(x_in, 16)
            scr = scratch.rearrange("(p i) c -> p i c", p=P)
            for b in range(NB):
                rows = slice(TPB * b, TPB * (b + 1))
                sp.wait_ge(solved, TPB * (b + 1))
                sp.dma_start(scr[:, rows, :], ukk[:, rows, :, :].rearrange("p i a c -> p i (a c)")
                             ).then_inc(scratch_out, 16)
            sp.wait_ge(scratch_out, 16 * NB)
            sp.wait_ge(consts, 1)
            groups = scratch.rearrange("(q g i) c -> q i g c", g=RG, i=SUB)
            with sp.Fori(0, NRG // SLOTS) as it:
                for b in range(SLOTS):
                    sp.wait_ge(m_psum, (it * SLOTS + b - SLOTS) * RG + 1 + FREE["m_psum"])
                    sp.dma_start(sub[0:SUB, b, :, :],
                                 groups[bass.ds(it * SLOTS + b, 1)].rearrange("o i g c -> (o i) g c")
                                 ).then_inc(sub_in[b], 16)
            sp.wait_ge(x_added, NB)

            def load_expert(e, s):
                loaded = ew_in[s]
                sp.dma_start(ew1[:, s, :], io["ew1"][bass.ds(e, 1)].rearrange("o d h -> (o d) h")).then_inc(loaded, 16)
                sp.dma_start(ew3[:, s, :], io["ew3"][bass.ds(e, 1)].rearrange("o d h -> (o d) h")).then_inc(loaded, 16)
                sp.dma_start(ew2[:, s, :, :],
                             io["ew2"][bass.ds(e, 1)].rearrange("o (j p) c -> (o p) j c", p=P)).then_inc(loaded, 16)

            load_expert(0, 0)
            load_expert(1, 1)
            with sp.Fori(1, EXPERTS // 2) as ep:
                for s in range(2):
                    sp.wait_ge(down_psum, ep * (2 * NB) - NB * (1 - s))
                    load_expert(ep * 2 + s, s)
            for b in range(NB):
                sp.wait_ge(fo_added, b + 1 + FREE["fo_added"])
                sp.dma_start(ov[:, TPB * b:TPB * (b + 1), :], x[:, TPB * b:TPB * (b + 1), :]).then_inc(y_out, 16)
            sp.wait_ge(y_out, 16 * NB)

        @block.gpsimd
        def _(pool):
            pool.sem_inc(pool_acc, FREE["pool_acc"])
            step = Steps(pool, pool_step)
            step(nc.gpsimd.memset(ident[:, :], 0.0))
            step(nc.gpsimd.affine_select(out=ident[:, :], in_=ident[:, :], compare_op=ALU.not_equal, fill=1.0,
                                         base=0, pattern=[[-1, P]], channel_multiplier=1))
            nc.gpsimd.tensor_copy(ident16[:, :], ident[:, :])
            nc.gpsimd.tensor_scalar(neg_ident[:, :], ident[:, :], -1.0, None, ALU.mult)
            for g in range(RG):
                nc.gpsimd.tensor_copy(eye4[:, g, :], ident[:, :])
            step(nc.gpsimd.memset(mask[:, :], 1.0))
            mask_v = mask[:, :].rearrange("p (h d) -> p h d", d=DH)
            step(nc.gpsimd.affine_select(out=mask_v, in_=mask_v, compare_op=ALU.is_ge, fill=0.0, base=0,
                                         pattern=[[-DH, HEADS], [0, DH]], channel_multiplier=1))
            step(nc.gpsimd.affine_select(out=mask_v, in_=mask_v, compare_op=ALU.is_ge, fill=0.0, base=DH - 1,
                                         pattern=[[DH, HEADS], [0, DH]], channel_multiplier=-1))
            for g in range(RG):
                nc.gpsimd.tensor_scalar(negmask[:, g, :], mask[:, :], -1.0, None, ALU.mult)
            nc.gpsimd.memset(ones[:, :], 1.0)
            nc.gpsimd.memset(zeros16[:, :], 0.0)
            nc.gpsimd.memset(sub[:, :, :, :], 0.0)
            nc.gpsimd.memset(yT[:, 0, :], 0.0)
            nc.gpsimd.memset(minus_half[:, :], -0.5)
            step(nc.gpsimd.memset(earlier[:, :, :], 1.0))
            nc.gpsimd.affine_select(out=earlier[:, :, :], in_=earlier[:, :, :], compare_op=ALU.is_gt, fill=0.0, base=0,
                                    pattern=[[1, EXPERTS], [-1, EXPERTS]],
                                    channel_multiplier=0).then_inc(consts, 1)

            def rsqrt_rows(k):
                pool.wait_ge(var_ready, k)
                nc.gpsimd.tensor_tensor(rstd[:, :], var[:, :], minus_half[:, 0:NT],
                                        ALU.pow).then_inc(rstd_ready, 1)

            pool.wait_ge(consts, 1)
            rsqrt_rows(1)
            pool.wait_ge(kss_ready, 1)
            step(nc.gpsimd.tensor_tensor(krn[:, :], kss[:, :], minus_half[:, :], ALU.pow))
            nc.gpsimd.tensor_scalar(krn[:, :], krn[:, :], 1e12, None, ALU.min).then_inc(krn_ready, 1)

            def query_keys(i):
                if i > 2:
                    pool.wait_ge(qdots_ready, i - 2)
                nc.gpsimd.tensor_tensor(qk[i % 2][:, 0:i, :], kaq[:, i, 1, :].unsqueeze(1).broadcast_to([P, i, P]),
                                        ukk[:, 0:i, 2, :], ALU.mult).then_inc(qk_ready, 1)

            def weigh_updates(i):
                pool.wait_ge(qdots_ready, i)
                pool.wait_ge(solved, i)
                for n, s0, s1 in pieces(i):
                    if n > 2:
                        pool.wait_ge(qprod_used, n - 2)
                    for a in range(2):
                        last = nc.gpsimd.tensor_tensor(
                            qprod[:, n % 2, 0:s1 - s0, a, :].rearrange("p s (h d) -> p s h d", d=DH),
                            ukk[:, s0:s1, a, :].rearrange("p s (h d) -> p s h d", d=DH),
                            qdots[:, i % 2, s0 * HEADS:s1 * HEADS].rearrange("p (s h) -> p s h", h=HEADS).unsqueeze(3)
                            .broadcast_to([P, s1 - s0, HEADS, DH]), ALU.mult)
                    last.then_inc(qprod_ready, 1)

            pool.wait_ge(kn_ready, 1)
            query_keys(1)
            for i in range(1, SUB):
                if i < SUB - 1:
                    query_keys(i + 1)
                weigh_updates(i)
            with pool.Fori(0, NRG // SLOTS) as it:
                for b in range(SLOTS):
                    pool.wait_ge(a_masked, (it * SLOTS + b) * 2 + 2)
                    nc.gpsimd.tensor_tensor(amat[:, b, :, :], amat[:, b, :, :], eye4[:, :, :],
                                            ALU.add).then_inc(a_ready, 1)
            rsqrt_rows(2)
            rsqrt_rows(3)
            pool.wait_ge(rstd_ready, 3)
            nc.gpsimd.memset(klm[DK:DK + 2, :], 1.0).then_inc(klm_ones, 1)
            pool.wait_ge(klm_ones, 1)
            nc.gpsimd.memset(klm[DK:DK + 1, :], MSPLIT).then_inc(klm_ones, 1)
            pool.wait_ge(klm_ones, 2)
            pool.wait_ge(xn_ready, 3 * NB)
            nc.gpsimd.tensor_tensor(x[:, :, :], x[:, :, :], bo[:, :].unsqueeze(1).broadcast_to([P, NT, P]),
                                    ALU.add).then_inc(bo_added, 1)
            with pool.Fori(0, NB) as qb:
                for h in range(HEADS):
                    pool.wait_ge(qh_ready, qb * HEADS + h + 1)
                    nc.gpsimd.tensor_tensor(qhm[0:DK, h, :], qhl[0:DK, h, :], zeros16[:, :],
                                            ALU.add).then_inc(qm_copied, 1)
                with pool.Fori(0, HEADS) as h:
                    u = qb * HEADS + h
                    for j in range(1, ADDS + 1):
                        pool.wait_ge(p_ready, u * STEPS + j + 1 + FREE["p_ready"])
                        if j == 1:
                            pool.wait_ge(keysum_ready, u + FREE["keysum_ready"])
                            first = pr[:, 0, :, :]
                        else:
                            pool.wait_ge(pool_acc, u * ADDS + j - 1 + FREE["pool_acc"])
                            first = acc[:, :, :]
                        nc.gpsimd.tensor_tensor(acc[:, :, :], first, pr[:, j % 4, :, :],
                                                ALU.add).then_inc(pool_acc, 1)
            rsqrt_rows(4)
            pool.wait_ge(xn_ready, 4 * NB)
            nc.gpsimd.tensor_tensor(x[:, :, :], x[:, :, :], b2[:, :].unsqueeze(1).broadcast_to([P, NT, P]),
                                    ALU.add).then_inc(b2_added, 1)

        @block.scalar
        def _(act):
            act.sem_inc(act1_ready, FREE["act1_ready"])
            act.sem_inc(p_ready, FREE["p_ready"])
            act.sem_inc(o_saved, FREE["o_saved"])
            act.sem_inc(ff_ready, FREE["ff_ready"])
            for dst, src in loads:
                act.dma_start(dst, src).then_inc(w_in, 16)
            act.wait_ge(w_in, 16 * len(loads))
            nc.scalar.activation(ab[:, :, :], ab[:, :, :], ACT.Exp, scale=-1.0).then_inc(ab_exp, 1)

            def copy_xnT(k, b):
                act.wait_ge(xnT_psum, NB * (k - 1) + b + 1)
                nc.scalar.activation(xnT[:, BT * b:BT * (b + 1)], bank(b), ACT.Copy).then_inc(xnT_ready, 1)

            for b in range(NB):
                copy_xnT(1, b)
                for i in range(TPB * b, TPB * (b + 1)):
                    act.wait_ge(qkv_psum, i + 1)
                    nc.scalar.activation(kaq[:, i, 1, :], bank(4 + i % 4)[:, 0:P], ACT.Copy)
                    nc.scalar.activation(kv[:, i, :], bank(4 + i % 4)[:, P:3 * P], ACT.Copy).then_inc(qkv_ready, 1)
            for i in range(SUB):
                act.wait_ge(qo_psum, i + 1)
                if i > 0:
                    act.wait_ge(qprod_used, pieces(i)[-1][0])
                    nc.scalar.activation(yT[:, i, :], ps[:, 2 * (i % 2), 0:P], ACT.Copy)
                nc.scalar.activation(qT[:, i, :], ps[:, 2 * (i % 2) + 1, 0:P], ACT.Copy).then_inc(qo_sbuf, 1)
            for b in range(NB):
                copy_xnT(2, b)
            act.wait_ge(shift_ready, 1)
            nc.scalar.activation(probs[:, :, :], probs[:, :, :], ACT.Exp).then_inc(gate_exp, 1)
            with act.Fori(0, EXPERTS) as e:
                for n in range(UP):
                    act.wait_ge(up_psum, e * UP + n + 1)
                    act.wait_ge(hid_ready, e * UP + n - 1 + FREE["hid_ready"])
                    nc.scalar.activation(act1[:, n % 2, :], bank(2 * (n % 2)), ACT.Silu).then_inc(act1_ready, 1)
            for b in range(NB):
                copy_xnT(3, b)
            for b in range(NB):
                act.wait_ge(kp_psum, b + 1)
                nc.scalar.activation(khh[:, BT * b:BT * (b + 1)], bank(b), ACT.Identity,
                                     bias=bk2[:, 0:1]).then_inc(kh_ready, 1)

            def save_output(u):
                act.wait_ge(pv_done, (u + 1) * STEPS + FREE["pv_done"])
                act.wait_ge(wo_ready, u + FREE["wo_ready"])
                nc.scalar.activation(osb[:, :], bank(OB), ACT.Copy).then_inc(o_saved, 1)

            def exps(u, prev, nxt):
                for j in range(STEPS):
                    act.wait_ge(st_ready, u * STEPS + j + 1)
                    act.wait_ge(pv_done, u * STEPS + j - 3 + FREE["pv_done"])
                    if j < 4:
                        act.wait_ge(pool_acc, u * ADDS - 3 + j + FREE["pool_acc"])
                    else:
                        act.wait_ge(pool_acc, u * ADDS + max(1, j - 4) + FREE["pool_acc"])
                    nc.scalar.activation(pr[:, j % 4, :, :], ps[:, 2 * (j % 2):2 * (j % 2) + 2, :],
                                         ACT.Exp).then_inc(p_ready, 1)
                    if j == 0 and prev:
                        save_output(u - 1)
                if not nxt:
                    save_output(u)

            with act.Fori(0, NB) as qb:
                for k in range(HEADS // 2):
                    act.wait_ge(q_psum, qb * (HEADS // 2) + k + 1)
                    for half in range(2):
                        rows = slice(DK * half, DK * (half + 1))
                        h = 2 * k + half
                        nc.scalar.activation(qhl[0:DK, h, :], ps[rows, k % 4, :], ACT.Identity,
                                             bias=bq[:, h:h + 1]).then_inc(qh_ready, 1)
                exps(qb * HEADS, False, True)
                with act.Fori(1, HEADS - 1) as h:
                    exps(qb * HEADS + h, True, True)
                exps(qb * HEADS + HEADS - 1, True, False)

            for b in range(NB):
                copy_xnT(4, b)
            with act.Fori(0, NB // 2) as it:
                for s in range(2):
                    for j in range(FF // P):
                        act.wait_ge(ff_psum, (it * 2 + s) * (FF // P) + j + 1)
                        nc.scalar.activation(ffT[:, s, j, :], bank(j), ACT.Relu,
                                             bias=b1[:, j:j + 1]).then_inc(ff_ready, 1)

        @block.vector
        def _(dve):
            V = nc.vector
            dve.sem_inc(y_ready, FREE["y_ready"])
            dve.sem_inc(hid_ready, FREE["hid_ready"])
            dve.sem_inc(down_added, FREE["down_added"])
            dve.sem_inc(keysum_ready, FREE["keysum_ready"])
            dve.sem_inc(mx_free, FREE["mx_free"])
            dve.sem_inc(wo_added, FREE["wo_added"])
            dve.sem_inc(fo_added, FREE["fo_added"])
            step = Steps(dve, dve_step)

            def layernorm(k):
                step(V.tensor_reduce(row_sum[:, :], x[:, :, :], AX.X, ALU.add))
                step(V.tensor_scalar(mean[:, :], row_sum[:, :], 1.0 / P, None, ALU.mult))
                step(V.tensor_tensor(xn[:, :, :], x[:, :, :], mean[:, :].unsqueeze(2).broadcast_to([P, NT, P]),
                                     ALU.subtract))
                step(V.tensor_tensor(work[:, :, :], xn[:, :, :], xn[:, :, :], ALU.mult))
                step(V.tensor_reduce(row_sum[:, :], work[:, :, :], AX.X, ALU.add))
                V.tensor_scalar(var[:, :], row_sum[:, :], 1.0 / P, EPS, ALU.mult, ALU.add).then_inc(var_ready, 1)
                dve.wait_ge(rstd_ready, k)
                for b in range(NB):
                    t = slice(TPB * b, TPB * (b + 1))
                    V.tensor_tensor(xn[:, t, :], xn[:, t, :], rstd[:, t].unsqueeze(2).broadcast_to([P, TPB, P]),
                                    ALU.mult).then_inc(xn_ready, 1)

            dve.wait_ge(x_in, 16)
            layernorm(1)
            dve.wait_ge(ab_exp, 1)
            step(V.tensor_scalar(ab[:, :, :], ab[:, :, :], 1.0, None, ALU.add))
            step(V.reciprocal(ab[:, :, :], ab[:, :, :]))
            step(V.tensor_scalar(ab[:, :, :], ab[:, :, :], 0.5, None, ALU.mult))
            V.tensor_scalar(wq[:, :], wq[:, :], DK ** -0.5, None, ALU.mult)
            step(V.tensor_scalar(bq[:, :], bq[:, :], DK ** -0.5, None, ALU.mult))
            dve.wait_ge(qkv_ready, NT)
            raw_k = kv[:, :, 0:P]
            step(V.tensor_tensor(work[:, :, :], raw_k, raw_k, ALU.mult))
            V.tensor_reduce(kss[:, :], work[:, :, :].rearrange("p i (h d) -> p (i h) d", d=DH), AX.X,
                            ALU.add).then_inc(kss_ready, 1)
            heads = lambda ap: ap.rearrange("p i (h d) -> p i h d", d=DH)
            per_head = lambda ap: ap.unsqueeze(1).unsqueeze(3).broadcast_to([P, NT, HEADS, DH])
            V.tensor_tensor(heads(ukk[:, :, 0, :]), heads(kv[:, :, P:2 * P]), per_head(ab[:, 1, :]), ALU.mult)
            dve.wait_ge(krn_ready, 1)
            V.tensor_tensor(heads(kn), heads(raw_k),
                            krn[:, :].rearrange("p (i h) -> p i h", h=HEADS).unsqueeze(3)
                            .broadcast_to([P, NT, HEADS, DH]), ALU.mult).then_inc(kn_ready, 1)
            dve.wait_ge(kn_ready, 1)
            step(V.tensor_tensor(heads(kaq[:, :, 0, :]), heads(kn), per_head(ab[:, 0, :]), ALU.mult))
            V.tensor_copy(ukk[:, :, 1, :], kaq[:, :, 0, :]).then_inc(solved, 1)
            dve.wait_ge(solved, 1)

            def solve(i):
                n = i * HEADS
                row = kaq[:, i, 0, :].unsqueeze(1).broadcast_to([P, i, P])
                step(V.tensor_tensor(prod1[:, 0:i, :], row, ukk[:, 0:i, 2, :], ALU.mult))
                step(V.tensor_reduce(dots[:, 0:n], prod1[:, 0:i, :].rearrange("p s (h d) -> p (s h) d", d=DH), AX.X,
                                     ALU.add))
                for a in range(2):
                    last = V.tensor_tensor(heads(prod2[:, 0:i, a * P:(a + 1) * P]), heads(ukk[:, 0:i, a, :]),
                                           dots[:, 0:n].rearrange("p (s h) -> p s h", h=HEADS).unsqueeze(3)
                                           .broadcast_to([P, i, HEADS, DH]), ALU.mult)
                step(last)
                step(V.tensor_reduce(corr[:, :], prod2[:, 0:i, :].rearrange("p s c -> p c s"), AX.X, ALU.add))
                own = ukk[:, i, 0:2, :].rearrange("p a c -> p (a c)")
                V.tensor_tensor(own, own, corr[:, :], ALU.subtract).then_inc(solved, 1)

            for i in range(1, SUB):
                solve(i)
                dve.wait_ge(qk_ready, i)
                if i > 2:
                    dve.wait_ge(qprod_ready, pieces(i - 1)[0][0] - 1)
                V.tensor_reduce(qdots[:, i % 2, 0:i * HEADS],
                                qk[i % 2][:, 0:i, :].rearrange("p s (h d) -> p (s h) d", d=DH), AX.X,
                                ALU.add).then_inc(qdots_ready, 1)
                dve.wait_ge(solved, i + 1)
            V.memset(mst[:, 0, :], 0.0).then_inc(m_ready, 1)

            def mask_transitions(c, b, half):
                dve.wait_ge(a_psum, c + 1)
                two = slice(2 * half, 2 * half + 2)
                V.tensor_tensor(amat[:, b, two, :], ps[:, b % 2, :].rearrange("p (g c) -> p g c", g=RG)[:, two, :],
                                negmask[:, 0:2, :], ALU.mult).then_inc(a_masked, 1)

            def add_outputs(c, b):
                dve.wait_ge(y_psum, c + 1)
                cols = yT[:, :, bass.ds(c * RG, RG)].rearrange("p i g -> p g i")
                V.tensor_tensor(cols, ps[:, 4 + b % 2, 0:RG * SUB].rearrange("p (g i) -> p g i", g=RG), cols,
                                ALU.add).then_inc(y_ready, 1)

            def states(c, b, first, last):
                for g in range(RG):
                    dve.wait_ge(m_psum, c * RG + g + 1 + FREE["m_psum"])
                    V.tensor_tensor(mst[:, (g + 1) % RG, :], ps[:, 2 + b % 2, g * P:(g + 1) * P], mask[:, :],
                                    ALU.mult).then_inc(m_ready, 1)
                    if g == 0 and not first:
                        add_outputs(c - 1, (b - 1) % SLOTS)
                    if g >= 2 and not last:
                        mask_transitions(c + 2, (b + 2) % SLOTS, g - 2)

            for c in range(2):
                for half in range(2):
                    mask_transitions(c, c, half)
            dve.wait_ge(qo_sbuf, SUB)
            for b in range(SLOTS):
                states(b, b, b == 0, False)
            with dve.Fori(1, NRG // SLOTS - 1) as it:
                for b in range(SLOTS):
                    states(it * SLOTS + b, b, False, False)
            for b in range(SLOTS):
                states(NRG - SLOTS + b, b, False, b >= 2)
            add_outputs(NRG - 1, SLOTS - 1)
            for b in range(NB):
                dve.wait_ge(proj_psum, b + 1)
                t = slice(TPB * b, TPB * (b + 1))
                V.tensor_tensor(x[:, t, :], ps[:, 4 + b, :].rearrange("p (t c) -> p t c", t=TPB), x[:, t, :],
                                ALU.add).then_inc(x_added, 1)
            dve.wait_ge(x_added, NB)
            layernorm(2)

            dve.wait_ge(gate_psum, 1)
            logits = ps[:, 4, 0:P].rearrange("p (t e) -> p t e", e=EXPERTS)
            over_e = lambda ap: ap.unsqueeze(2).broadcast_to([P, NT, EXPERTS])
            step(V.tensor_reduce(r1[:, :], logits, AX.X, ALU.max))
            V.tensor_tensor(probs[:, :, :], logits, over_e(r1[:, :]), ALU.subtract).then_inc(shift_ready, 1)
            dve.wait_ge(gate_exp, 1)
            step(V.tensor_reduce(r1[:, :], probs[:, :, :], AX.X, ALU.add))
            step(V.reciprocal(r1[:, :], r1[:, :]))
            step(V.tensor_tensor(probs[:, :, :], probs[:, :, :], over_e(r1[:, :]), ALU.mult))
            other = probs[:, :, :].unsqueeze(2).broadcast_to([P, NT, EXPERTS, EXPERTS])
            own = probs[:, :, :].unsqueeze(3).broadcast_to([P, NT, EXPERTS, EXPERTS])
            V.tensor_tensor(cmp_gt[:, :, :, :], other, own, ALU.is_gt)
            step(V.tensor_tensor(cmp_eq[:, :, :, :], other, own, ALU.is_equal))
            step(V.tensor_tensor(cmp_eq[:, :, :, :], cmp_eq[:, :, :, :],
                                 earlier[:, :, :].unsqueeze(1).broadcast_to([P, NT, EXPERTS, EXPERTS]), ALU.mult))
            step(V.tensor_tensor(cmp_gt[:, :, :, :], cmp_gt[:, :, :, :], cmp_eq[:, :, :, :], ALU.add))
            step(V.tensor_reduce(rank[:, :, :], cmp_gt[:, :, :, :], AX.X, ALU.add))
            step(V.scalar_tensor_tensor(gatew[:, :, :], rank[:, :, :], float(TOPK), probs[:, :, :], ALU.is_lt,
                                        ALU.mult))

            def add_expert(e, b):
                n = e * NB + b
                dve.wait_ge(down_psum, n + 1)
                dve.wait_ge(down_added, n + FREE["down_added"])
                for t in range(TPB):
                    i = TPB * b + t
                    last = V.scalar_tensor_tensor(x[:, i, :], ps[:, 4 + b % 2, t * P:(t + 1) * P],
                                                  gatew[:, i, bass.ds(e, 1)], x[:, i, :], ALU.mult, ALU.add)
                last.then_inc(down_added, 1)

            with dve.Fori(0, EXPERTS) as e:
                for n in range(UP):
                    dve.wait_ge(gt_psum, e * UP + n + 1)
                    dve.wait_ge(act1_ready, e * UP + n + 1 + FREE["act1_ready"])
                    V.tensor_tensor(hidT[:, (n // 2) % 2, n % 2, :], ps[:, 2 * (n % 2) + 1, :], act1[:, n % 2, :],
                                    ALU.mult).then_inc(hid_ready, 1)
                    if n % 2 == 0 and n > 0:
                        add_expert(e, n // 2 - 1)
                add_expert(e, NB - 1)
            dve.wait_ge(down_added, EXPERTS * NB + FREE["down_added"])
            layernorm(3)

            for b in range(NB):
                dve.wait_ge(kh_ready, b + 1)
                cols = slice(BT * b, BT * (b + 1))
                V.scalar_tensor_tensor(klm[0:DK, cols], ps[0:DK, b, :], bk2[0:DK, 0:1], khh[0:DK, cols], ALU.add,
                                       ALU.subtract).then_inc(kl_ready, 1)
            for n in range(2):
                dve.wait_ge(vp_psum, n + 1)
                V.tensor_tensor(vt[:, 8 * n:8 * (n + 1), :], ps[:, 4 + n, :].rearrange("p (t d) -> p t d", d=DK),
                                bv[:, :].unsqueeze(1).broadcast_to([P, 8, DK]), ALU.add).then_inc(v_ready, 1)

            def chunk_max(u, m):
                dve.wait_ge(mx_ready, u * NCH + m + 1)
                V.tensor_reduce(cmax[:, m // NB, m % NB:m % NB + 1], bank(MX + m % 2), AX.X,
                                ALU.max).then_inc(mx_free, 1)

            def split_max(u):
                dve.wait_ge(mx_free, (u + 1) * NCH + FREE["mx_free"])
                V.tensor_reduce(nmax[:, :], cmax[:, :, :], AX.X, ALU.max, negate=True).then_inc(max_step, 1)
                dve.wait_ge(max_step, u * 2 + 1)
                V.tensor_scalar(m16[:, :, 0], nmax[:, :], 1.0 / MSPLIT, None, ALU.mult).then_inc(max_step, 1)
                dve.wait_ge(max_step, u * 2 + 2)
                V.scalar_tensor_tensor(m16[:, :, 1], m16[:, :, 0], -MSPLIT, nmax[:, :], ALU.mult,
                                       ALU.add).then_inc(rowmax_ready, 1)

            def place_max(u, h):
                dve.wait_ge(tr_ready, u + 1)
                V.tensor_copy(qhm[DK:DK + 2, bass.ds(h, 1), :].rearrange("p o c -> p (o c)"),
                              small16[DK:DK + 2, 0:BT]).then_inc(t2_ready, 1)

            def finish_sum(u):
                dve.wait_ge(pool_acc, (u + 1) * ADDS + FREE["pool_acc"])
                V.tensor_tensor(keysum[:, :], acc[:, 0, :], acc[:, 1, :], ALU.add).then_inc(keysum_ready, 1)

            def read_denominator(u):
                dve.wait_ge(den_ready, u + 1)
                V.reciprocal(rden[:, :], ps[:, SM, 0:TPB]).then_inc(den_read, 1)

            def add_head(u, qb):
                dve.wait_ge(wo_ready, u + 1 + FREE["wo_ready"])
                dve.wait_ge(wo_added, u + FREE["wo_added"])
                dve.wait_ge(den_read, u + 1)
                for t in range(TPB):
                    row = x[:, bass.ds(qb * TPB + t, 1), :].rearrange("p o c -> p (o c)")
                    last = V.scalar_tensor_tensor(row, ps[:, SM, t * P:(t + 1) * P], rden[:, t:t + 1], row, ALU.mult,
                                                  ALU.add)
                last.then_inc(wo_added, 1)

            def head(u, qb, h, prev, nxt):
                m = 0
                for j in range(STEPS):
                    if nxt:
                        for _ in range(MAX_CHUNKS[j]):
                            chunk_max(u + 1, m)
                            m += 1
                    if j == 1 and prev:
                        finish_sum(u - 1)
                    if j == 3 and prev:
                        read_denominator(u - 1)
                    if j == 4 and prev:
                        add_head(u - 1, qb)
                    if j == 6 and nxt:
                        split_max(u + 1)
                    if j == 7 and nxt:
                        place_max(u + 1, h + 1)
                if not nxt:
                    finish_sum(u)
                    read_denominator(u)
                    add_head(u, qb)

            dve.wait_ge(bo_added, 1)
            with dve.Fori(0, NB) as qb:
                for k in range(HEADS // 2):
                    dve.wait_ge(qh_ready, qb * HEADS + 2 * k + 2)
                    for half in range(2):
                        rows = slice(DK * half, DK * (half + 1))
                        h = 2 * k + half
                        V.scalar_tensor_tensor(qhl[DK:2 * DK, h, :], ps[rows, k % 4, :], bq[:, h:h + 1],
                                               qhl[0:DK, h, :], ALU.add, ALU.subtract).then_inc(ql_ready, 1)
                u0 = qb * HEADS
                for m in range(NCH):
                    chunk_max(u0, m)
                split_max(u0)
                place_max(u0, 0)
                head(u0, qb, 0, False, True)
                with dve.Fori(1, HEADS - 1) as h:
                    head(u0 + h, qb, h, True, True)
                head(u0 + HEADS - 1, qb, HEADS - 1, True, False)

            dve.wait_ge(wo_added, NB * HEADS + FREE["wo_added"])
            layernorm(4)
            dve.wait_ge(b2_added, 1)
            with dve.Fori(0, NB // 2) as it:
                for s in range(2):
                    dve.wait_ge(fo_psum, it * 2 + s + 1)
                    t = bass.ds((it * 2 + s) * TPB, TPB)
                    V.tensor_tensor(x[:, t, :], ps[:, 4 + s, :].rearrange("p (t c) -> p t c", t=TPB), x[:, t, :],
                                    ALU.add).then_inc(fo_added, 1)

        @block.tensor
        def _(pe):
            mm = nc.tensor.matmul
            pe.sem_inc(m_psum, FREE["m_psum"])
            pe.sem_inc(pv_done, FREE["pv_done"])
            pe.sem_inc(wo_ready, FREE["wo_ready"])

            def transpose_xn(k, b):
                pe.wait_ge(xn_ready, NB * (k - 1) + b + 1)
                for t in range(TPB):
                    last = nc.tensor.transpose(ps[:, b, t * P:(t + 1) * P], xn[:, TPB * b + t, :], ident[:, :])
                last.then_inc(xnT_psum, 1)

            def tile(i):
                return xnT[:, i * P:(i + 1) * P]

            pe.wait_ge(consts, 1)
            pe.wait_ge(w_in, 16 * len(loads))
            for b in range(NB):
                transpose_xn(1, b)
            for b in range(NB):
                pe.wait_ge(xnT_ready, b + 1)
                for i in range(TPB * b, TPB * (b + 1)):
                    if i >= 4:
                        pe.wait_ge(qkv_ready, i - 3)
                    mm(ps[:, 4 + i % 4, 0:3 * P], tile(i), wqkv[:, :], start=True, stop=True).then_inc(qkv_psum, 1)
            pe.wait_ge(qkv_ready, NT)
            for i in range(SUB):
                o_bank, q_bank = ps[:, 2 * (i % 2), 0:P], ps[:, 2 * (i % 2) + 1, 0:P]
                if i < 2:
                    pe.wait_ge(xnT_ready, NB)
                else:
                    pe.wait_ge(qo_sbuf, i - 1)
                mm(q_bank, kaq[:, i, 1, :], ident[:, :], start=True, stop=(i == 0)).then_inc(qo_psum, 1)
                for n, s0, s1 in pieces(i):
                    pe.wait_ge(qprod_ready, n)
                    for s in range(s0, s1):
                        mm(o_bank, qprod[:, n % 2, s - s0, 0, :], ident[:, :], start=(s == 0), stop=(s == i - 1))
                        last = mm(q_bank, qprod[:, n % 2, s - s0, 1, :], neg_ident[:, :], start=False,
                                  stop=(s == i - 1))
                    last.then_inc(qprod_used, 1)
            pe.wait_ge(qo_sbuf, SUB)

            def operand(b, g, k):
                return sub[:, b, g, k * P:(k + 1) * P]

            def transitions(c, b, gs):
                for g in gs:
                    last = mm(ps[:, b % 2, g * P:(g + 1) * P], operand(b, g, 1), operand(b, g, 2), start=True,
                              stop=True)
                if gs[-1] == RG - 1:
                    last.then_inc(a_psum, 1)

            def additions(b, gs):
                for g in gs:
                    mm(ps[:, 2 + b % 2, g * P:(g + 1) * P], operand(b, g, 2), operand(b, g, 0), start=(g == 0),
                       stop=False, skip_group_check=True)

            def advance(c, b, turn, transitions_follow=True, additions_follow=True):
                pe.wait_ge(a_ready, c + 1)
                pe.wait_ge(y_ready, c - 1 + FREE["y_ready"])
                for g in range(RG):
                    pe.wait_ge(m_ready, c * RG + g + 1)
                    mm(ps[:, 2 + b % 2, g * P:(g + 1) * P], amat[:, b, g, :], mst[:, g, :], start=False,
                       stop=True, skip_group_check=True).then_inc(m_psum, 1)
                    last = mm(ps[:, 4 + b % 2, g * SUB:(g + 1) * SUB], mst[:, g, :],
                              qT[:, :, bass.ds(c * RG + g, 1)].rearrange("p i o -> p (i o)"), start=True, stop=True)
                    if g == RG - 1:
                        last.then_inc(y_psum, 1)
                    if g == 0 and transitions_follow:
                        pe.wait_ge(sub_in[(b + 2) % SLOTS], (turn + (b + 2) // SLOTS + 1) * 16)
                        pe.wait_ge(a_masked, c * 2 + 2)
                    if g < 2 and transitions_follow:
                        transitions(c + 2, (b + 2) % SLOTS, [2 * g, 2 * g + 1])
                    if g >= 2 and additions_follow:
                        additions((b + 1) % SLOTS, [2 * g - 4, 2 * g - 3])

            for c in range(2):
                pe.wait_ge(sub_in[c], 16)
                transitions(c, c, [0, 1, 2, 3])
            additions(0, [0, 1, 2, 3])
            with pe.Fori(0, NRG // SLOTS - 1) as it:
                for b in range(SLOTS):
                    advance(it * SLOTS + b, b, it)
            for b in range(SLOTS):
                advance(NRG - SLOTS + b, b, NRG // SLOTS - 1, b < 2, b < SLOTS - 1)
            pe.wait_ge(y_ready, NRG + FREE["y_ready"])
            for b in range(NB):
                for t in range(TPB):
                    last = mm(ps[:, 4 + b, t * P:(t + 1) * P], yT[:, TPB * b + t, :], wproj[:, :], start=True, stop=True)
                last.then_inc(proj_psum, 1)

            for b in range(NB):
                transpose_xn(2, b)
            pe.wait_ge(xnT_ready, 2 * NB)
            for i in range(NT):
                last = mm(ps[:, 4, i * EXPERTS:(i + 1) * EXPERTS], tile(i), gate[:, :], start=True, stop=True)
            last.then_inc(gate_psum, 1)

            def expert_down(e, b, s):
                n = e * NB + b
                pe.wait_ge(hid_ready, n * 2 + 2 + FREE["hid_ready"])
                pe.wait_ge(down_added, n - 1 + FREE["down_added"])
                for t in range(TPB):
                    for j in range(HID // P):
                        last = mm(ps[:, 4 + b % 2, t * P:(t + 1) * P], hidT[:, b % 2, j, t * P:(t + 1) * P],
                                  ew2[:, s, j, :], start=(j == 0), stop=(j == HID // P - 1))
                last.then_inc(down_psum, 1)

            with pe.Fori(0, EXPERTS // 2) as ep:
                for s in range(2):
                    e = ep * 2 + s
                    pe.wait_ge(ew_in[s], ep * 48 + 48)
                    for n in range(UP):
                        b, j = n // 2, n % 2
                        src = xnT[:, BT * b:BT * (b + 1)]
                        pe.wait_ge(act1_ready, e * UP + n - 1 + FREE["act1_ready"])
                        mm(bank(2 * j), ew1[:, s, j * P:(j + 1) * P], src, start=True, stop=True).then_inc(up_psum, 1)
                        pe.wait_ge(hid_ready, e * UP + n - 1 + FREE["hid_ready"])
                        mm(bank(2 * j + 1), ew3[:, s, j * P:(j + 1) * P], src, start=True,
                           stop=True).then_inc(gt_psum, 1)
                        if j == 0 and n > 0:
                            expert_down(e, b - 1, s)
                    expert_down(e, NB - 1, s)

            for b in range(NB):
                transpose_xn(3, b)
            for b in range(NB):
                pe.wait_ge(xnT_ready, 2 * NB + b + 1)
                mm(bank(b), wk2[:, :, :].rearrange("p a d -> p (a d)"), xnT[:, BT * b:BT * (b + 1)], start=True,
                   stop=True).then_inc(kp_psum, 1)
            for n in range(2):
                for t in range(8):
                    last = mm(ps[:, 4 + n, t * DK:(t + 1) * DK], tile(8 * n + t), wv[:, :], start=True, stop=True)
                last.then_inc(vp_psum, 1)
            pe.wait_ge(kl_ready, NB)
            pe.wait_ge(v_ready, 2)
            pe.wait_ge(klm_ones, 2)

            def scores(u, h, j, a):
                keys = slice((2 * j + a) * P, (2 * j + a + 1) * P)
                dst = bank(2 * (j % 2) + a)
                pe.wait_ge(p_ready, u * STEPS + j - 1 + FREE["p_ready"])
                mm(dst, khh[:, keys], qhl[:, bass.ds(h, 1), :].rearrange("p o c -> p (o c)"), start=True, stop=False)
                last = mm(dst, klm[:, keys], qhm[:, bass.ds(h, 1), :].rearrange("p o c -> p (o c)"), start=False,
                          stop=True)
                if a == 1:
                    last.then_inc(st_ready, 1)

            def max_scores(u, h, m):
                pe.wait_ge(mx_free, u * NCH + m - 1 + FREE["mx_free"])
                qt, kb = m // NB, m % NB
                mm(bank(MX + m % 2), qhl[:, bass.ds(h, 1), qt * P:(qt + 1) * P].rearrange("p o c -> p (o c)"),
                   khh[:, kb * BT:(kb + 1) * BT], start=True, stop=True).then_inc(mx_ready, 1)

            def turn_max(u):
                pe.wait_ge(rowmax_ready, u + 1)
                pe.wait_ge(wo_added, u - 1 + FREE["wo_added"])
                for qt in range(TPB):
                    last = nc.tensor.transpose(small16[DK:DK + 2, qt * P:(qt + 1) * P], m16[:, qt, :], ident16[:, :])
                last.then_inc(tr_ready, 1)

            def weigh_values(u, j):
                pe.wait_ge(p_ready, u * STEPS + j + 1 + FREE["p_ready"])
                if j == 0:
                    pe.wait_ge(o_saved, u + FREE["o_saved"])
                for a in range(2):
                    last = mm(ps[DK * a:DK * (a + 1), OB, :], vt[:, 2 * j + a, :], pr[:, j % 4, a, :], start=(j == 0),
                              stop=(j == STEPS - 1))
                last.then_inc(pv_done, 1)

            def denominator(u):
                pe.wait_ge(keysum_ready, u + 1 + FREE["keysum_ready"])
                for t in range(TPB):
                    last = mm(ps[:, SM, t:t + 1], keysum[:, t * P:(t + 1) * P], ones[:, :], start=True, stop=True)
                last.then_inc(den_ready, 1)

            def project_head(u, h):
                pe.wait_ge(den_read, u + 1)
                pe.wait_ge(o_saved, u + 1 + FREE["o_saved"])
                for t in range(TPB):
                    last = mm(ps[:, SM, t * P:(t + 1) * P], osb[:, t * P:(t + 1) * P],
                              wo2[:, bass.ds(h, 1), :].rearrange("p o c -> p (o c)"), start=True, stop=True)
                last.then_inc(wo_ready, 1)

            def head(u, h, prev, nxt):
                m = 0
                for j in range(STEPS):
                    if j == 0:
                        pe.wait_ge(t2_ready, u + 1)
                    chunks = list(range(m, m + MAX_CHUNKS[j])) if nxt else []
                    m += len(chunks)
                    scores(u, h, j, 0)
                    if chunks:
                        max_scores(u + 1, h + 1, chunks[0])
                    scores(u, h, j, 1)
                    if j == 7 and nxt:
                        turn_max(u + 1)
                    if chunks:
                        max_scores(u + 1, h + 1, chunks[1])
                    if j > 0:
                        weigh_values(u, j - 1)
                    elif prev:
                        weigh_values(u - 1, STEPS - 1)
                    if len(chunks) > 2:
                        max_scores(u + 1, h + 1, chunks[2])
                    if j == 2 and prev:
                        denominator(u - 1)
                    if j == 4 and prev:
                        project_head(u - 1, h - 1)
                if not nxt:
                    weigh_values(u, STEPS - 1)
                    denominator(u)
                    project_head(u, h)

            with pe.Fori(0, NB) as qb:
                u0 = qb * HEADS
                for k in range(HEADS // 2):
                    if k < 4:
                        pe.wait_ge(p_ready, u0 * STEPS + FREE["p_ready"])
                    else:
                        pe.wait_ge(ql_ready, qb * HEADS + 2 * (k - 3))
                    mm(bank(k % 4), wq[:, k * P:(k + 1) * P], xnT[:, bass.ds(qb * BT, BT)], start=True,
                       stop=True).then_inc(q_psum, 1)
                pe.wait_ge(ql_ready, qb * HEADS + HEADS)
                pe.wait_ge(qm_copied, qb * HEADS + HEADS)
                for m in range(NCH):
                    max_scores(u0, 0, m)
                turn_max(u0)
                head(u0, 0, False, True)
                with pe.Fori(1, HEADS - 1) as h:
                    head(u0 + h, h, True, True)
                head(u0 + HEADS - 1, HEADS - 1, True, False)

            for b in range(NB):
                transpose_xn(4, b)
            NF = FF // P
            pe.wait_ge(xnT_ready, 4 * NB)
            with pe.Fori(0, NB // 2) as it:
                for s in range(2):
                    n = it * 2 + s
                    for j in range(NF):
                        pe.wait_ge(ff_ready, n * NF + j - 3 + FREE["ff_ready"])
                        mm(bank(j), w1[:, j * P:(j + 1) * P], xnT[:, bass.ds(n * BT, BT)], start=True,
                           stop=True).then_inc(ff_psum, 1)
                    pe.wait_ge(ff_ready, n * NF + NF + FREE["ff_ready"])
                    pe.wait_ge(fo_added, n - 1 + FREE["fo_added"])
                    for t in range(TPB):
                        for j in range(NF):
                            last = mm(ps[:, 4 + s, t * P:(t + 1) * P], ffT[:, s, j, t * P:(t + 1) * P], w2[:, j, :],
                                      start=(j == 0), stop=(j == NF - 1))
                    last.then_inc(fo_psum, 1)


def kernel(**inputs):
    import numpy as np
    import concourse.bacc as bacc
    from concourse.bass_utils import run_bass_kernel_spmd

    g = {name: np.asarray(a) for name, a in inputs.items()}
    arrays = {
        "x": g["L0_attn_x"],
        "wqkv": np.concatenate([g["L0_attn_Wq"].T, g["L0_attn_Wk"].T, g["L0_attn_Wv"].T], axis=1),
        "wproj": g["L0_attn_Wproj"].T,
        "alpha": g["L0_attn_alpha_raw"], "beta": g["L0_attn_beta_raw"],
        "gate": g["L0_ffn_gate_w"].T, "ew1": g["L0_ffn_w1"], "ew2": g["L0_ffn_w2"], "ew3": g["L0_ffn_w3"],
        "wq": g["L1_attn_Wq"], "bq": g["L1_attn_bq"].reshape(HEADS, DK).T,
        "wk": g["L1_attn_Wk"], "bk": g["L1_attn_bk"].reshape(DK, 1),
        "wv": g["L1_attn_Wv"], "bv": g["L1_attn_bv"], "wo": g["L1_attn_Wo"], "bo": g["L1_attn_bo"],
        "w1": g["L1_ffn_W1"], "b1": g["L1_ffn_b1"].reshape(FF // P, P).T,
        "w2": g["L1_ffn_W2"], "b2": g["L1_ffn_b2"],
    }
    arrays = {name: np.ascontiguousarray(a) for name, a in arrays.items()}
    nc = bacc.Bacc("TRN2", target_bir_lowering=False, num_devices=1)
    io = {name: nc.dram_tensor("in_" + name, a.shape, mybir.dt.from_np(a.dtype), kind="ExternalInput").ap()
          for name, a in arrays.items()}
    shape = arrays["x"].shape
    out = nc.dram_tensor("out", shape, F32, kind="ExternalOutput").ap()
    build(nc, io, out)
    result = run_bass_kernel_spmd(nc, [{"in_" + name: a for name, a in arrays.items()}], core_ids=[0])
    return result.results[0]["out"]
```

```python
from contextlib import ExitStack

import concourse.bass as bass
from concourse import mybir

ALU = mybir.AluOpType
ACT = mybir.ActivationFunctionType
AX = mybir.AxisListType
F32 = mybir.dt.float32
F16 = mybir.dt.float16

P = 128
T = 2048
NT = T // P
NB = 4
BT = T // NB
TPB = NT // NB
HEADS = 16
DH = P // HEADS
SUB = NT
NSUB = T // SUB
RG = 4
NRG = NSUB // RG
SLOTS = 4
EXPERTS, HID, TOPK = 8, 256, 2
DK = 64
FF = 512
KT = T // P
QPIECE = 8
STEPS = KT // 2
WSCALE = 16.0
MSPLIT = 64.0
EPS = 1e-5
MAX_CHUNKS = [3, 3, 2, 3, 2, 3, 0, 0]
FREE = {"y_ready": 2, "act1_ready": 2, "hid_ready": 2, "down_added": 3, "p_ready": 2, "pv_done": 4,
        "pool_acc": 7, "sum_step": 2, "mx_free": 2, "o_saved": 1, "o_summed": 2, "o_normal": 2, "wo_added": 1,
        "ff_ready": 4, "fo_added": 2, "m_psum": 16}


class Steps:

    def __init__(self, engine, sem):
        self.engine, self.sem, self.count = engine, sem, 0

    def __call__(self, instruction):
        instruction.then_inc(self.sem, 1)
        self.count = self.count + 1
        self.engine.wait_ge(self.sem, self.count)


def build(nc, io, out):
    with ExitStack() as ctx:
        def sb(name, shape, dt=F32, scope=ctx):
            return scope.enter_context(nc.sbuf_tensor(name, shape, dt))

        def sem(name):
            return ctx.enter_context(nc.semaphore(name))

        x = sb("x", [P, NT, P])
        xn = sb("xn", [P, NT, P])
        xnT = sb("xnT", [P, T])
        work = sb("work", [P, NT, P])
        stats = sb("stats", [P, NT, 6])
        moments = sb("moments", [P, NT, 2])
        var = sb("var", [P, NT])
        rstd = sb("rstd", [P, NT])
        ident = sb("ident", [P, P])
        neg_ident = sb("neg_ident", [P, P])
        wscale = sb("wscale", [P, 1])
        zero = sb("zero", [P, 1])
        ident16 = sb("ident16", [P, P], F16)
        mask = sb("mask", [P, P])
        negmask = sb("negmask", [P, RG, P])
        eye4 = sb("eye4", [P, RG, P])
        ones16 = sb("ones16", [P, DK], F16)
        minus_half = sb("minus_half", [P, NT])
        earlier = sb("earlier", [P, EXPERTS, EXPERTS])
        wqkv = sb("wqkv", [P, 3 * P])
        wproj = sb("wproj", [P, P])
        ab = sb("ab", [P, 2, HEADS])
        gate = sb("gate", [P, EXPERTS])
        wq = sb("wq", [P, HEADS * DK])
        bq = sb("bq", [DK, HEADS])
        wk2 = sb("wk2", [P, 2, DK])
        bk2 = sb("bk2", [P, 1])
        wv = sb("wv", [P, DK])
        bv = sb("bv", [P, DK])
        wo = sb("wo", [P, HEADS // 2, P])
        bo = sb("bo", [P, P])
        w1 = sb("w1", [P, FF])
        b1 = sb("b1", [P, FF // P])
        w2 = sb("w2", [P, FF // P, P])
        b2 = sb("b2", [P, P])

        a_scope = ExitStack()
        sa_ = lambda name, shape, dt=F32: sb(name, shape, dt, a_scope)
        kaq = sa_("kaq", [P, NT, 2, P])
        kv = sa_("kv", [P, NT, 2 * P])
        ukk = sa_("ukk", [P, NT, 3, P])
        dots = sa_("dots", [P, NT * HEADS])
        qdots = sa_("qdots", [P, 2, NT * HEADS])
        qprod = sa_("qprod", [P, 2, QPIECE, 2, P])
        kss = sa_("kss", [P, NT * HEADS])
        krn = sa_("krn", [P, NT * HEADS])
        sub = sa_("sub", [P, SLOTS, RG, 3 * P])
        amat = sa_("amat", [P, SLOTS, RG, P])
        mst = sa_("mst", [P, RG, P])
        qT = sa_("qT", [P, NT, P])
        yT = sa_("yT", [P, NT, P])
        kn = ukk[:, :, 2, :]
        prod1 = work
        sub_flat = sub[:, :, :, :].rearrange("p b g c -> p (b g c)")
        kprod = [kv[:, :, :], sub_flat[:, 0:NT * 2 * P].rearrange("p (i c) -> p i c", i=NT)]
        qk = [xn[:, :, :], xnT[:, :].rearrange("p (i c) -> p i c", c=P)]
        a_scope.close()

        ew13 = sb("ew13", [P, 2, 2, HID])
        whigh = sb("whigh", [P, 2, 2, HID], F16)
        wlow = sb("wlow", [P, 2, 2, HID], F16)
        xhigh = sb("xhigh", [P, T], F16)
        xlow = sb("xlow", [P, T], F16)
        ew2 = sb("ew2", [P, 2, HID // P, P])
        act1 = sb("act1", [P, 2, BT])
        hidT = sb("hidT", [P, 2, HID // P, BT])
        r1 = sb("r1", [P, NT])
        probs = sb("probs", [P, NT, EXPERTS])
        cmp_gt = sb("cmp_gt", [P, NT, EXPERTS, EXPERTS])
        cmp_eq = sb("cmp_eq", [P, NT, EXPERTS, EXPERTS])
        rank = sb("rank", [P, NT, EXPERTS])
        gatew = sb("gatew", [P, NT, EXPERTS])
        khh = sb("khh", [P, T], F16)
        klm = sb("klm", [DK + 2, T], F16)
        vt = sb("vt", [P, KT, DK])
        wqp = sb("wqp", [P, 2 * DK])
        bqp = sb("bqp", [DK, 2])
        qhl = sb("qhl", [P, HEADS, BT], F16)
        qhm = sb("qhm", [DK + 2, HEADS, BT], F16)
        pr = sb("pr", [P, 4, 2, BT])
        acc = sb("acc", [P, 2, BT])
        keysum = sb("keysum", [P, BT])
        keysum16 = sb("keysum16", [P, 2, BT], F16)
        oeven = sb("oeven", [P, BT])
        oodd = sb("oodd", [P, BT])
        opair = sb("opair", [P, BT])
        cmax = sb("cmax", [P, TPB, NB])
        nmax = sb("nmax", [P, TPB])
        m16 = sb("m16", [P, TPB, 2], F16)
        ffT = sb("ffT", [P, 2, FF // P, BT])

        ps = ctx.enter_context(nc.psum_tensor("ps", [P, 8, BT], F32))

        def bank(b):
            return ps[:, b, :]

        MX, OB, SM = 4, 6, 7
        small16 = ps[:, MX + 1, :].bitcast(F16)

        scratch = nc.dram_tensor("scratch", [T, 3 * P], F32, kind="Internal").ap()

        (w_first, w_in, consts, pool_step, dve_step, xn_ready, xnT_psum, xnT_ready, var_ready, rstd_ready,
         ab_exp, qkv_psum, qkv_ready, kss_ready, krn_ready, kn_ready, ab_ready, ak_ready, alpha_k_copied,
         u_ready, solved, scratch_out, qk_ready, qdots_ready, qprod_ready, qprod_used, kprod_ready, kk_summed,
         sub_zeroed, qo_psum, qo_sbuf, a_psum, a_masked, a_ready, m_psum, m_ready, y_psum, y_ready, proj_psum,
         x_added, gate_psum, shift_ready, gate_exp, xhigh_ready, xlow_ready, ew_step, ew_split, up_psum,
         gt_psum, act1_ready, hid_ready, down_psum, down_added, kp_psum, kh_ready, kl_ready, vp_psum, v_ready,
         bo_added, wq_ready, q_psum, qh_ready, ql_ready, qm_copied, st_ready, p_ready, pv_done, pool_acc,
         sum_step, keysum_ready, mx_ready, mx_free, max_step, rowmax_ready, tr_ready, t2_ready, o_saved,
         o_summed, den_ready, den_inverted, o_normal, wo_ready, wo_added, b2_added, ff_psum, ff_ready,
         fo_psum, fo_added, y_out, klm_ones) = (sem(n) for n in """
            w_first w_in consts pool_step dve_step xn_ready xnT_psum xnT_ready var_ready rstd_ready ab_exp
            qkv_psum qkv_ready kss_ready krn_ready kn_ready ab_ready ak_ready alpha_k_copied u_ready solved
            scratch_out qk_ready qdots_ready qprod_ready qprod_used kprod_ready kk_summed sub_zeroed qo_psum
            qo_sbuf a_psum a_masked a_ready m_psum m_ready y_psum y_ready proj_psum x_added gate_psum
            shift_ready gate_exp xhigh_ready xlow_ready ew_step ew_split up_psum gt_psum act1_ready hid_ready
            down_psum down_added kp_psum kh_ready kl_ready vp_psum v_ready bo_added wq_ready q_psum qh_ready
            ql_ready qm_copied st_ready p_ready pv_done pool_acc sum_step keysum_ready mx_ready mx_free
            max_step rowmax_ready tr_ready t2_ready o_saved o_summed den_ready den_inverted o_normal wo_ready
            wo_added b2_added ff_psum ff_ready fo_psum fo_added y_out klm_ones""".split())
        x_in = [sem(f"x_in{b}") for b in range(NB)]
        sub_in = [sem(f"sub_in{b}") for b in range(SLOTS)]
        ew_in = [sem(f"ew_in{b}") for b in range(2)]
        block = ctx.enter_context(nc.Block())

        xv = io["x"].rearrange("o (p i) c -> (o p) i c", p=P)
        ov = out.rearrange("o (p i) c -> (o p) i c", p=P)
        loads = [(wqkv[:, :], io["wqkv"]), (ab[:, 0, :], io["alpha"].partition_broadcast(P)),
                 (ab[:, 1, :], io["beta"].partition_broadcast(P)),
                 (wproj[:, :], io["wproj"]), (gate[:, :], io["gate"]), (wq[:, :], io["wq"]),
                 (bq[:, :], io["bq"]), (wk2[:, 0, :], io["wk"]), (wk2[:, 1, :], io["wk"]),
                 (bk2[0:DK, :], io["bk"]), (bk2[DK:2 * DK, :], io["bk"]), (wv[:, :], io["wv"]),
                 (bv[:, :], io["bv"].partition_broadcast(P)),
                 (wo[:, :, :], io["wo"].rearrange("(k p) m -> p k m", p=P)),
                 (bo[:, :], io["bo"].partition_broadcast(P)),
                 (w1[:, :], io["w1"]), (b1[:, :], io["b1"]),
                 (w2[:, :, :], io["w2"].rearrange("(j p) m -> p j m", p=P)),
                 (b2[:, :], io["b2"].partition_broadcast(P))]
        W_REST = 16 * (len(loads) - 3)
        UP = 2 * NB
        NF = FF // P
        NCH = TPB * NB
        ADDS = STEPS - 1

        def attention(engine, pair):
            last_k = HEADS // 2 - 1

            def rest(qb):
                with engine.Fori(1, last_k) as k:
                    pair(qb, k, qb, k + 1, False, False)

            pair(0, 0, 0, 1, True, False)
            with engine.Fori(0, NB - 1) as qb:
                rest(qb)
                pair(qb, last_k, qb + 1, 0, False, False)
                pair(qb + 1, 0, qb + 1, 1, False, False)
            rest(NB - 1)
            pair(NB - 1, last_k, None, None, False, True)

        def pieces(i):
            n = 1 + sum(-(-j // QPIECE) for j in range(1, i))
            return [(n + k, s, min(s + QPIECE, i)) for k, s in enumerate(range(0, i, QPIECE))]

        @block.sync
        def _(sp):
            for b in range(NB):
                sp.dma_start(x[:, TPB * b:TPB * (b + 1), :], xv[:, TPB * b:TPB * (b + 1), :]).then_inc(x_in[b], 16)
            for dst, src in loads[3:]:
                sp.dma_start(dst, src).then_inc(w_in, 16)
            scr = scratch.rearrange("(p i) c -> p i c", p=P)
            for b in range(NB):
                rows = slice(TPB * b, TPB * (b + 1))
                sp.wait_ge(solved, TPB * (b + 1))
                sp.dma_start(scr[:, rows, :], ukk[:, rows, :, :].rearrange("p i a c -> p i (a c)")
                             ).then_inc(scratch_out, 16)
            sp.wait_ge(scratch_out, 16 * NB)
            sp.wait_ge(sub_zeroed, 1)
            groups = scratch.rearrange("(q g i) c -> q i g c", g=RG, i=SUB)
            with sp.Fori(0, NRG // SLOTS) as it:
                for b in range(SLOTS):
                    sp.wait_ge(m_psum, (it * SLOTS + b - SLOTS) * RG + 1 + FREE["m_psum"])
                    sp.dma_start(sub[0:SUB, b, :, :],
                                 groups[bass.ds(it * SLOTS + b, 1)].rearrange("o i g c -> (o i) g c")
                                 ).then_inc(sub_in[b], 16)
            sp.wait_ge(x_added, NB)

            def load_expert(e, s):
                loaded = ew_in[s]
                sp.dma_start(ew13[:, s, 0, :],
                             io["ew1"][bass.ds(e, 1)].rearrange("o d h -> (o d) h")).then_inc(loaded, 16)
                sp.dma_start(ew13[:, s, 1, :],
                             io["ew3"][bass.ds(e, 1)].rearrange("o d h -> (o d) h")).then_inc(loaded, 16)
                sp.dma_start(ew2[:, s, :, :],
                             io["ew2"][bass.ds(e, 1)].rearrange("o (j p) c -> (o p) j c", p=P)).then_inc(loaded, 16)

            load_expert(0, 0)
            load_expert(1, 1)
            with sp.Fori(1, EXPERTS // 2) as ep:
                for s in range(2):
                    sp.wait_ge(down_psum, ep * (2 * NB) - NB * (1 - s))
                    sp.wait_ge(ew_split, ep * 2 + s - 1)
                    load_expert(ep * 2 + s, s)
            for b in range(NB):
                sp.wait_ge(fo_added, b + 1 + FREE["fo_added"])
                sp.dma_start(ov[:, TPB * b:TPB * (b + 1), :], x[:, TPB * b:TPB * (b + 1), :]).then_inc(y_out, 16)
            sp.wait_ge(y_out, 16 * NB)

        @block.gpsimd
        def _(pool):
            pool.sem_inc(pool_acc, FREE["pool_acc"])
            step = Steps(pool, pool_step)
            step(nc.gpsimd.memset(ident[:, :], 0.0))
            step(nc.gpsimd.affine_select(out=ident[:, :], in_=ident[:, :], compare_op=ALU.not_equal, fill=1.0,
                                         base=0, pattern=[[-1, P]], channel_multiplier=1))
            nc.gpsimd.tensor_copy(ident16[:, :], ident[:, :])
            nc.gpsimd.tensor_scalar(neg_ident[:, :], ident[:, :], -1.0, None, ALU.mult)
            for g in range(RG):
                nc.gpsimd.tensor_copy(eye4[:, g, :], ident[:, :])
            step(nc.gpsimd.memset(mask[:, :], 1.0))
            mask_v = mask[:, :].rearrange("p (h d) -> p h d", d=DH)
            step(nc.gpsimd.affine_select(out=mask_v, in_=mask_v, compare_op=ALU.is_ge, fill=0.0, base=0,
                                         pattern=[[-DH, HEADS], [0, DH]], channel_multiplier=1))
            step(nc.gpsimd.affine_select(out=mask_v, in_=mask_v, compare_op=ALU.is_ge, fill=0.0, base=DH - 1,
                                         pattern=[[DH, HEADS], [0, DH]], channel_multiplier=-1))
            for g in range(RG):
                nc.gpsimd.tensor_scalar(negmask[:, g, :], mask[:, :], -1.0, None, ALU.mult)
            nc.gpsimd.memset(ones16[:, :], 1.0)
            nc.gpsimd.memset(yT[:, 0, :], 0.0)
            nc.gpsimd.memset(wscale[:, :], WSCALE)
            nc.gpsimd.memset(zero[:, :], 0.0)
            nc.gpsimd.memset(minus_half[:, :], -0.5)
            step(nc.gpsimd.memset(earlier[:, :, :], 1.0))
            nc.gpsimd.affine_select(out=earlier[:, :, :], in_=earlier[:, :, :], compare_op=ALU.is_gt, fill=0.0, base=0,
                                    pattern=[[1, EXPERTS], [-1, EXPERTS]],
                                    channel_multiplier=0).then_inc(consts, 1)

            def rsqrt_rows(k, b):
                pool.wait_ge(var_ready, NB * (k - 1) + b + 1)
                t = slice(TPB * b, TPB * (b + 1))
                nc.gpsimd.tensor_tensor(rstd[:, t], var[:, t], minus_half[:, t], ALU.pow).then_inc(rstd_ready, 1)

            pool.wait_ge(consts, 1)
            for b in range(NB):
                rsqrt_rows(1, b)

            pool.wait_ge(w_in, W_REST)
            nc.gpsimd.tensor_scalar(wq[:, :], wq[:, :], DK ** -0.5, None, ALU.mult)
            nc.gpsimd.tensor_scalar(bq[:, :], bq[:, :], DK ** -0.5, None, ALU.mult)
            pool.wait_ge(ab_ready, 1)
            pool.wait_ge(qkv_ready, NT)
            nc.gpsimd.tensor_tensor(ukk[:, :, 0, :].rearrange("p i (h d) -> p i h d", d=DH),
                                    kv[:, :, P:2 * P].rearrange("p i (h d) -> p i h d", d=DH),
                                    ab[:, 1, :].unsqueeze(1).unsqueeze(3).broadcast_to([P, NT, HEADS, DH]),
                                    ALU.mult).then_inc(u_ready, 1)

            def query_keys(i):
                if i > 2:
                    pool.wait_ge(qdots_ready, i - 2)
                nc.gpsimd.tensor_tensor(qk[i % 2][:, 0:i, :], kaq[:, i, 1, :].unsqueeze(1).broadcast_to([P, i, P]),
                                        ukk[:, 0:i, 2, :], ALU.mult).then_inc(qk_ready, 1)

            def weigh_updates(i):
                pool.wait_ge(qdots_ready, i)
                pool.wait_ge(solved, i)
                for n, s0, s1 in pieces(i):
                    if n > 2:
                        pool.wait_ge(qprod_used, n - 2)
                    for a in range(2):
                        last = nc.gpsimd.tensor_tensor(
                            qprod[:, n % 2, 0:s1 - s0, a, :].rearrange("p s (h d) -> p s h d", d=DH),
                            ukk[:, s0:s1, a, :].rearrange("p s (h d) -> p s h d", d=DH),
                            qdots[:, i % 2, s0 * HEADS:s1 * HEADS].rearrange("p (s h) -> p s h", h=HEADS).unsqueeze(3)
                            .broadcast_to([P, s1 - s0, HEADS, DH]), ALU.mult)
                    last.then_inc(qprod_ready, 1)

            pool.wait_ge(kn_ready, 1)
            query_keys(1)
            for i in range(1, SUB):
                if i < SUB - 1:
                    query_keys(i + 1)
                weigh_updates(i)
            with pool.Fori(0, NRG // SLOTS) as it:
                for b in range(SLOTS):
                    pool.wait_ge(a_masked, (it * SLOTS + b) * 2 + 2)
                    nc.gpsimd.tensor_tensor(amat[:, b, :, :], amat[:, b, :, :], eye4[:, :, :],
                                            ALU.add).then_inc(a_ready, 1)
            for b in range(NB):
                rsqrt_rows(2, b)

            def split_expert(e, s, turn, first=False):
                pool.wait_ge(ew_in[s], turn * 48 + 48)
                if not first:
                    pool.wait_ge(gt_psum, (e - 1) * UP)
                shape = [P, 2, HID]
                nc.gpsimd.tensor_tensor(ew13[:, s, :, :], ew13[:, s, :, :],
                                        wscale[:, :].unsqueeze(2).broadcast_to(shape), ALU.mult).then_inc(ew_step, 1)
                pool.wait_ge(ew_step, e * 2 + 1)
                nc.gpsimd.tensor_tensor(whigh[:, s, :, :], ew13[:, s, :, :],
                                        zero[:, :].unsqueeze(2).broadcast_to(shape), ALU.add).then_inc(ew_step, 1)
                pool.wait_ge(ew_step, e * 2 + 2)
                nc.gpsimd.tensor_tensor(wlow[:, s, :, :], ew13[:, s, :, :], whigh[:, s, :, :],
                                        ALU.subtract).then_inc(ew_split, 1)

            split_expert(0, 0, 0, True)
            for b in range(NB):
                pool.wait_ge(xhigh_ready, b + 1)
                cols = slice(BT * b, BT * (b + 1))
                nc.gpsimd.tensor_tensor(xlow[:, cols], xnT[:, cols], xhigh[:, cols],
                                        ALU.subtract).then_inc(xlow_ready, 1)
            split_expert(1, 1, 0, True)
            with pool.Fori(1, EXPERTS // 2) as ep:
                for s in range(2):
                    split_expert(ep * 2 + s, s, ep)
            for b in range(NB):
                rsqrt_rows(3, b)
            pool.wait_ge(rstd_ready, 3 * NB)
            nc.gpsimd.memset(klm[DK:DK + 2, :], 1.0).then_inc(klm_ones, 1)
            pool.wait_ge(klm_ones, 1)
            nc.gpsimd.memset(klm[DK:DK + 1, :], MSPLIT).then_inc(klm_ones, 1)
            pool.wait_ge(klm_ones, 2)
            pool.wait_ge(xn_ready, 3 * NB)
            pool.wait_ge(w_in, W_REST)
            nc.gpsimd.tensor_tensor(x[:, :, :], x[:, :, :], bo[:, :].unsqueeze(1).broadcast_to([P, NT, P]),
                                    ALU.add).then_inc(bo_added, 1)

            def sum_probabilities(u, steps):
                for j in steps:
                    pool.wait_ge(p_ready, u * STEPS + j + 1 + FREE["p_ready"])
                    if j == 1:
                        pool.wait_ge(sum_step, u * 2 - 1 + FREE["sum_step"])
                        first = pr[:, 0, :, :]
                    else:
                        pool.wait_ge(pool_acc, u * ADDS + j - 1 + FREE["pool_acc"])
                        first = acc[:, :, :]
                    nc.gpsimd.tensor_tensor(acc[:, :, :], first, pr[:, j % 4, :, :], ALU.add).then_inc(pool_acc, 1)

            def add_b2(b):
                pool.wait_ge(xn_ready, 3 * NB + b + 1)
                t = slice(TPB * b, TPB * (b + 1))
                nc.gpsimd.tensor_tensor(x[:, t, :], x[:, t, :], b2[:, :].unsqueeze(1).broadcast_to([P, TPB, P]),
                                        ALU.add).then_inc(b2_added, 1)

            with pool.Fori(0, NB * HEADS - 1) as u:
                sum_probabilities(u, range(1, ADDS + 1))
            sum_probabilities(NB * HEADS - 1, (1, 2))
            for b in range(NB - 1):
                rsqrt_rows(4, b)
            sum_probabilities(NB * HEADS - 1, range(3, ADDS + 1))
            for b in range(NB - 1):
                add_b2(b)
            rsqrt_rows(4, NB - 1)
            add_b2(NB - 1)

        @block.scalar
        def _(act):
            act.sem_inc(act1_ready, FREE["act1_ready"])
            act.sem_inc(p_ready, FREE["p_ready"])
            act.sem_inc(o_saved, FREE["o_saved"])
            act.sem_inc(ff_ready, FREE["ff_ready"])
            for dst, src in loads[:3]:
                act.dma_start(dst, src).then_inc(w_first, 16)
            act.wait_ge(w_first, 16 * 3)
            nc.scalar.activation(ab[:, :, :], ab[:, :, :], ACT.Exp, scale=-1.0).then_inc(ab_exp, 1)

            def copy_xnT(k, b, src=None):
                act.wait_ge(xnT_psum, NB * (k - 1) + b + 1)
                nc.scalar.activation(xnT[:, BT * b:BT * (b + 1)], bank(b if src is None else src),
                                     ACT.Copy).then_inc(xnT_ready, 1)

            copy_xnT(1, 0)
            for b in range(NB):
                if b < NB - 1:
                    copy_xnT(1, b + 1)
                for i in range(TPB * b, TPB * (b + 1)):
                    act.wait_ge(qkv_psum, i + 1)
                    nc.scalar.activation(kaq[:, i, 1, :], bank(4 + i % 4)[:, 0:P], ACT.Copy)
                    nc.scalar.activation(work[:, i, :], bank(4 + i % 4)[:, P:2 * P], ACT.Square)
                    nc.scalar.activation(kv[:, i, :], bank(4 + i % 4)[:, P:3 * P], ACT.Copy).then_inc(qkv_ready, 1)
            act.wait_ge(kss_ready, 1)
            nc.scalar.activation(krn[:, :], kss[:, :], ACT.Sqrt).then_inc(krn_ready, 1)
            act.wait_ge(ak_ready, 1)
            nc.scalar.activation(ukk[:, 0:2, 1, :], kaq[:, 0:2, 0, :], ACT.Copy).then_inc(solved, 1)
            nc.scalar.activation(ukk[:, 2:NT, 1, :], kaq[:, 2:NT, 0, :], ACT.Copy).then_inc(alpha_k_copied, 1)
            for i in range(SUB):
                act.wait_ge(qo_psum, i + 1)
                if i > 0:
                    act.wait_ge(qprod_used, pieces(i)[-1][0])
                    nc.scalar.activation(yT[:, i, :], ps[:, 2 * (i % 2), 0:P], ACT.Copy)
                nc.scalar.activation(qT[:, i, :], ps[:, 2 * (i % 2) + 1, 0:P], ACT.Copy).then_inc(qo_sbuf, 1)
            for b in range(NB):
                copy_xnT(2, b)
                act.wait_ge(xnT_ready, NB + b + 1)
                nc.scalar.activation(xhigh[:, BT * b:BT * (b + 1)], xnT[:, BT * b:BT * (b + 1)],
                                     ACT.Copy).then_inc(xhigh_ready, 1)
            act.wait_ge(w_in, W_REST)
            act.wait_ge(shift_ready, 1)
            nc.scalar.activation(probs[:, :, :], probs[:, :, :], ACT.Exp).then_inc(gate_exp, 1)
            with act.Fori(0, EXPERTS) as e:
                for n in range(UP):
                    act.wait_ge(up_psum, e * UP + n + 1)
                    act.wait_ge(hid_ready, e * UP + n - 1 + FREE["hid_ready"])
                    nc.scalar.activation(act1[:, n % 2, :], bank(2 * (n % 2)), ACT.Silu,
                                         scale=1.0 / WSCALE).then_inc(act1_ready, 1)
            for b in range(NB):
                copy_xnT(3, b)
            for b in range(NB):
                act.wait_ge(kp_psum, b + 1)
                nc.scalar.activation(khh[:, BT * b:BT * (b + 1)], bank(b), ACT.Identity,
                                     bias=bk2[:, 0:1]).then_inc(kh_ready, 1)

            def save_output(u, half):
                act.wait_ge(pv_done, (u + 1) * STEPS + FREE["pv_done"])
                act.wait_ge(o_summed, u - 1 + FREE["o_summed"])
                rows = slice(DK * half, DK * (half + 1))
                nc.scalar.activation(oeven[rows, :], ps[0:DK, OB, :], ACT.Copy)
                nc.scalar.activation(oodd[rows, :], ps[DK:2 * DK, OB, :], ACT.Copy).then_inc(o_saved, 1)

            def save_queries(n, k):
                act.wait_ge(q_psum, n + 1)
                for half in range(2):
                    head = qhl[0:DK, bass.ds(2 * k + half, 1), :].rearrange("p o c -> p (o c)")
                    nc.scalar.activation(head, ps[DK * half:DK * (half + 1), SM, :], ACT.Identity,
                                         bias=bqp[:, half:half + 1]).then_inc(qh_ready, 1)

            def copy_queries(n, k, half):
                act.wait_ge(qh_ready, 2 * n + half + 1)
                src = qhl[0:DK, bass.ds(2 * k + half, 1), :].rearrange("p o c -> p (o c)")
                dst = qhm[0:DK, bass.ds(2 * k + half, 1), :].rearrange("p o c -> p (o c)")
                nc.scalar.activation(dst, src, ACT.Copy).then_inc(qm_copied, 1)

            def place_max(u, h):
                act.wait_ge(tr_ready, u + 1)
                nc.scalar.activation(qhm[DK:DK + 2, bass.ds(h, 1), :].rearrange("p o c -> p (o c)"),
                                     small16[DK:DK + 2, 0:BT], ACT.Copy).then_inc(t2_ready, 1)

            def exps(u, prev_half, n, next_head, next_k):
                for j in range(STEPS):
                    if j == 7 and next_head is not None:
                        place_max(u + 1, next_head)
                    act.wait_ge(st_ready, u * STEPS + j + 1)
                    act.wait_ge(pv_done, u * STEPS + j - 3 + FREE["pv_done"])
                    if j < 4:
                        act.wait_ge(pool_acc, u * ADDS - 3 + j + FREE["pool_acc"])
                    else:
                        act.wait_ge(pool_acc, u * ADDS + max(1, j - 4) + FREE["pool_acc"])
                    nc.scalar.activation(pr[:, j % 4, :, :], ps[:, 2 * (j % 2):2 * (j % 2) + 2, :],
                                         ACT.Exp).then_inc(p_ready, 1)
                    if j == 0 and prev_half is not None:
                        save_output(u - 1, prev_half)
                    if next_k is not None:
                        if j == 1:
                            save_queries(n + 1, next_k)
                        if j in (3, 4):
                            copy_queries(n + 1, next_k, j - 3)

            def pair(qb, k, next_qb, next_k, first, last):
                n = qb * (HEADS // 2) + k
                exps(2 * n, None if first else 1, n, 2 * k + 1, next_k)
                exps(2 * n + 1, 0, n, None if last else 2 * next_k, None)

            save_queries(0, 0)
            copy_queries(0, 0, 0)
            copy_queries(0, 0, 1)
            place_max(0, 0)
            attention(act, pair)
            save_output(NB * HEADS - 1, 1)

            for b in range(NB - 1):
                copy_xnT(4, b)
            for n in range(NB):
                for j in range(NF):
                    act.wait_ge(ff_psum, n * NF + j + 1)
                    nc.scalar.activation(ffT[:, n % 2, j, :], bank(j), ACT.Relu,
                                         bias=b1[:, j:j + 1]).then_inc(ff_ready, 1)
                if n == 0:
                    copy_xnT(4, NB - 1, OB)

        @block.vector
        def _(dve):
            V = nc.vector
            dve.sem_inc(y_ready, FREE["y_ready"])
            dve.sem_inc(hid_ready, FREE["hid_ready"])
            dve.sem_inc(down_added, FREE["down_added"])
            dve.sem_inc(sum_step, FREE["sum_step"])
            dve.sem_inc(mx_free, FREE["mx_free"])
            dve.sem_inc(o_summed, FREE["o_summed"])
            dve.sem_inc(o_normal, FREE["o_normal"])
            dve.sem_inc(wo_added, FREE["wo_added"])
            dve.sem_inc(fo_added, FREE["fo_added"])
            step = Steps(dve, dve_step)

            def row_stats(k, b):
                tokens = range(TPB * b, TPB * (b + 1))
                for i in tokens:
                    last = V.bn_stats(stats[:, i, :], x[:, i, :])
                step(last)
                for i in tokens:
                    last = V.bn_aggr(moments[:, i, :], stats[:, i, :])
                step(last)
                t = slice(TPB * b, TPB * (b + 1))
                V.tensor_scalar(var[:, t], moments[:, t, 1], 1.0, EPS, ALU.mult, ALU.add).then_inc(var_ready, 1)

            def normalise(k, b):
                dve.wait_ge(rstd_ready, NB * (k - 1) + b + 1)
                for i in range(TPB * b, TPB * (b + 1)):
                    last = V.tensor_scalar(xn[:, i, :], x[:, i, :], moments[:, i, 0:1], rstd[:, i:i + 1],
                                           ALU.subtract, ALU.mult)
                last.then_inc(xn_ready, 1)

            for b in range(NB):
                dve.wait_ge(x_in[b], 16)
                row_stats(1, b)
                if b > 0:
                    normalise(1, b - 1)
            normalise(1, NB - 1)
            dve.wait_ge(ab_exp, 1)
            step(V.tensor_scalar(ab[:, :, :], ab[:, :, :], 1.0, None, ALU.add))
            step(V.reciprocal(ab[:, :, :], ab[:, :, :]))
            V.tensor_scalar(ab[:, :, :], ab[:, :, :], 0.5, None, ALU.mult).then_inc(ab_ready, 1)
            dve.wait_ge(ab_ready, 1)
            dve.wait_ge(qkv_ready, NT)
            raw_k = kv[:, :, 0:P]
            V.tensor_reduce(kss[:, :], work[:, :, :].rearrange("p i (h d) -> p (i h) d", d=DH), AX.X,
                            ALU.add).then_inc(kss_ready, 1)
            heads = lambda ap: ap.rearrange("p i (h d) -> p i h d", d=DH)
            per_head = lambda ap: ap.unsqueeze(1).unsqueeze(3).broadcast_to([P, NT, HEADS, DH])
            dve.wait_ge(krn_ready, 1)
            step(V.tensor_scalar(krn[:, :], krn[:, :], 1e-12, None, ALU.max))
            step(V.reciprocal(krn[:, :], krn[:, :]))
            step(V.tensor_tensor(dots[:, :], krn[:, :], krn[:, :], ALU.mult))
            step(V.tensor_tensor(dots[:, :], dots[:, :], kss[:, :], ALU.mult))
            step(V.tensor_scalar(dots[:, :], dots[:, :], -0.5, 1.5, ALU.mult, ALU.add))
            step(V.tensor_tensor(krn[:, :], krn[:, :], dots[:, :], ALU.mult))
            step(V.tensor_scalar(krn[:, :], krn[:, :], 1e12, None, ALU.min))
            V.tensor_tensor(heads(kn), heads(raw_k),
                            krn[:, :].rearrange("p (i h) -> p i h", h=HEADS).unsqueeze(3)
                            .broadcast_to([P, NT, HEADS, DH]), ALU.mult).then_inc(kn_ready, 1)
            dve.wait_ge(kn_ready, 1)
            V.tensor_tensor(heads(kaq[:, :, 0, :]), heads(kn), per_head(ab[:, 0, :]), ALU.mult).then_inc(ak_ready, 1)
            dve.wait_ge(ak_ready, 1)

            def key_dots(i):
                row = kaq[:, i, 0, :].unsqueeze(1).broadcast_to([P, i, P])
                step(V.tensor_tensor(prod1[:, 0:i, :], row, ukk[:, 0:i, 2, :], ALU.mult))
                step(V.tensor_reduce(dots[:, 0:i * HEADS], prod1[:, 0:i, :].rearrange("p s (h d) -> p (s h) d", d=DH),
                                     AX.X, ALU.add))

            def products(i, s0, s1):
                for a in range(2):
                    last = V.tensor_tensor(heads(kprod[1 - i % 2][:, s0:s1, a * P:(a + 1) * P]),
                                           heads(ukk[:, s0:s1, a, :]),
                                           dots[:, s0 * HEADS:s1 * HEADS].rearrange("p (s h) -> p s h", h=HEADS)
                                           .unsqueeze(3).broadcast_to([P, s1 - s0, HEADS, DH]), ALU.mult)
                last.then_inc(kprod_ready, 1)

            key_dots(1)
            dve.wait_ge(u_ready, 1)
            dve.wait_ge(solved, 1)
            for i in range(1, SUB):
                products(i, i - 1, i)
                dve.wait_ge(qk_ready, i)
                if i > 2:
                    dve.wait_ge(qprod_ready, pieces(i - 1)[0][0] - 1)
                V.tensor_reduce(qdots[:, i % 2, 0:i * HEADS],
                                qk[i % 2][:, 0:i, :].rearrange("p s (h d) -> p (s h) d", d=DH), AX.X,
                                ALU.add).then_inc(qdots_ready, 1)
                if i < SUB - 1:
                    dve.wait_ge(kprod_ready, 2 * i - 1)
                    key_dots(i + 1)
                    products(i + 1, 0, i)
                if i == SUB - 1:
                    dve.wait_ge(kk_summed, i - 1)
                    V.memset(sub[:, :, :, :], 0.0).then_inc(sub_zeroed, 1)
                dve.wait_ge(kk_summed, i)
                if i == 2:
                    dve.wait_ge(alpha_k_copied, 1)
                own = ukk[:, i, 0:2, :].rearrange("p a c -> p (a c)")
                V.tensor_tensor(own, own, ps[:, 4 + i % 2, 0:2 * P], ALU.subtract).then_inc(solved, 1)
                dve.wait_ge(solved, i + 1)
            V.memset(mst[:, 0, :], 0.0).then_inc(m_ready, 1)

            def mask_transitions(c, b, half):
                dve.wait_ge(a_psum, c + 1)
                two = slice(2 * half, 2 * half + 2)
                V.tensor_tensor(amat[:, b, two, :], ps[:, b % 2, :].rearrange("p (g c) -> p g c", g=RG)[:, two, :],
                                negmask[:, 0:2, :], ALU.mult).then_inc(a_masked, 1)

            def add_outputs(c, b):
                dve.wait_ge(y_psum, c + 1)
                cols = yT[:, :, bass.ds(c * RG, RG)].rearrange("p i g -> p g i")
                V.tensor_tensor(cols, ps[:, 4 + b % 2, 0:RG * SUB].rearrange("p (g i) -> p g i", g=RG), cols,
                                ALU.add).then_inc(y_ready, 1)

            def states(c, b, first, last):
                for g in range(RG):
                    dve.wait_ge(m_psum, c * RG + g + 1 + FREE["m_psum"])
                    V.tensor_tensor(mst[:, (g + 1) % RG, :], ps[:, 2 + b % 2, g * P:(g + 1) * P], mask[:, :],
                                    ALU.mult).then_inc(m_ready, 1)
                    if g == 0 and not first:
                        add_outputs(c - 1, (b - 1) % SLOTS)
                    if g >= 2 and not last:
                        mask_transitions(c + 2, (b + 2) % SLOTS, g - 2)

            for c in range(2):
                for half in range(2):
                    mask_transitions(c, c, half)
            dve.wait_ge(qo_sbuf, SUB)
            for b in range(SLOTS):
                states(b, b, b == 0, False)
            with dve.Fori(1, NRG // SLOTS - 1) as it:
                for b in range(SLOTS):
                    states(it * SLOTS + b, b, False, False)
            for b in range(SLOTS):
                states(NRG - SLOTS + b, b, False, b >= 2)
            add_outputs(NRG - 1, SLOTS - 1)
            for b in range(NB):
                dve.wait_ge(proj_psum, b + 1)
                t = slice(TPB * b, TPB * (b + 1))
                V.tensor_tensor(x[:, t, :], ps[:, 4 + b, :].rearrange("p (t c) -> p t c", t=TPB), x[:, t, :],
                                ALU.add).then_inc(x_added, 1)
                dve.wait_ge(x_added, b + 1)
                row_stats(2, b)
                if b > 0:
                    normalise(2, b - 1)
            normalise(2, NB - 1)

            dve.wait_ge(gate_psum, 1)
            logits = ps[:, 4, 0:P].rearrange("p (t e) -> p t e", e=EXPERTS)
            over_e = lambda ap: ap.unsqueeze(2).broadcast_to([P, NT, EXPERTS])
            step(V.tensor_reduce(r1[:, :], logits, AX.X, ALU.max))
            V.tensor_tensor(probs[:, :, :], logits, over_e(r1[:, :]), ALU.subtract).then_inc(shift_ready, 1)
            dve.wait_ge(gate_exp, 1)
            step(V.tensor_reduce(r1[:, :], probs[:, :, :], AX.X, ALU.add))
            step(V.reciprocal(r1[:, :], r1[:, :]))
            step(V.tensor_tensor(probs[:, :, :], probs[:, :, :], over_e(r1[:, :]), ALU.mult))
            other = probs[:, :, :].unsqueeze(2).broadcast_to([P, NT, EXPERTS, EXPERTS])
            own = probs[:, :, :].unsqueeze(3).broadcast_to([P, NT, EXPERTS, EXPERTS])
            V.tensor_tensor(cmp_gt[:, :, :, :], other, own, ALU.is_gt)
            step(V.tensor_tensor(cmp_eq[:, :, :, :], other, own, ALU.is_equal))
            step(V.tensor_tensor(cmp_eq[:, :, :, :], cmp_eq[:, :, :, :],
                                 earlier[:, :, :].unsqueeze(1).broadcast_to([P, NT, EXPERTS, EXPERTS]), ALU.mult))
            step(V.tensor_tensor(cmp_gt[:, :, :, :], cmp_gt[:, :, :, :], cmp_eq[:, :, :, :], ALU.add))
            step(V.tensor_reduce(rank[:, :, :], cmp_gt[:, :, :, :], AX.X, ALU.add))
            step(V.scalar_tensor_tensor(gatew[:, :, :], rank[:, :, :], float(TOPK), probs[:, :, :], ALU.is_lt,
                                        ALU.mult))
            step(V.tensor_scalar(gatew[:, :, :], gatew[:, :, :], 1.0 / WSCALE, None, ALU.mult))

            def add_expert(e, b):
                n = e * NB + b
                dve.wait_ge(down_psum, n + 1)
                dve.wait_ge(down_added, n + FREE["down_added"])
                for t in range(TPB):
                    i = TPB * b + t
                    last = V.scalar_tensor_tensor(x[:, i, :], ps[:, 4 + b % 2, t * P:(t + 1) * P],
                                                  gatew[:, i, bass.ds(e, 1)], x[:, i, :], ALU.mult, ALU.add)
                last.then_inc(down_added, 1)

            def expert(e, last=False):
                for n in range(UP):
                    dve.wait_ge(gt_psum, e * UP + n + 1)
                    dve.wait_ge(act1_ready, e * UP + n + 1 + FREE["act1_ready"])
                    V.tensor_tensor(hidT[:, (n // 2) % 2, n % 2, :], ps[:, 2 * (n % 2) + 1, :], act1[:, n % 2, :],
                                    ALU.mult).then_inc(hid_ready, 1)
                    if n % 2 == 0 and n > 0:
                        add_expert(e, n // 2 - 1)
                    if n % 2 == 1 and n > 1 and last:
                        normalise_added(n // 2 - 1)
                add_expert(e, NB - 1)

            def normalise_added(b):
                dve.wait_ge(down_added, (EXPERTS - 1) * NB + b + 1 + FREE["down_added"])
                row_stats(3, b)
                if b > 0:
                    normalise(3, b - 1)

            with dve.Fori(0, EXPERTS - 1) as e:
                expert(e)
            expert(EXPERTS - 1, last=True)
            normalise_added(NB - 1)
            normalise(3, NB - 1)

            for b in range(NB):
                dve.wait_ge(kh_ready, b + 1)
                cols = slice(BT * b, BT * (b + 1))
                V.scalar_tensor_tensor(klm[0:DK, cols], ps[0:DK, b, :], bk2[0:DK, 0:1], khh[0:DK, cols], ALU.add,
                                       ALU.subtract).then_inc(kl_ready, 1)
            for n in range(2):
                dve.wait_ge(vp_psum, n + 1)
                V.tensor_tensor(vt[:, 8 * n:8 * (n + 1), :], ps[:, 4 + n, :].rearrange("p (t d) -> p t d", d=DK),
                                bv[:, :].unsqueeze(1).broadcast_to([P, 8, DK]), ALU.add).then_inc(v_ready, 1)

            def chunk_max(u, m):
                dve.wait_ge(mx_ready, u * NCH + m + 1)
                V.tensor_reduce(cmax[:, m // NB, m % NB:m % NB + 1], bank(MX + m % 2), AX.X,
                                ALU.max).then_inc(mx_free, 1)

            def split_max(u):
                dve.wait_ge(mx_free, (u + 1) * NCH + FREE["mx_free"])
                V.tensor_reduce(nmax[:, :], cmax[:, :, :], AX.X, ALU.max, negate=True).then_inc(max_step, 1)
                dve.wait_ge(max_step, u * 2 + 1)
                V.tensor_scalar(m16[:, :, 0], nmax[:, :], 1.0 / MSPLIT, None, ALU.mult).then_inc(max_step, 1)
                dve.wait_ge(max_step, u * 2 + 2)
                V.scalar_tensor_tensor(m16[:, :, 1], m16[:, :, 0], -MSPLIT, nmax[:, :], ALU.mult,
                                       ALU.add).then_inc(rowmax_ready, 1)

            def finish_sum(u):
                dve.wait_ge(pool_acc, (u + 1) * ADDS + FREE["pool_acc"])
                V.tensor_tensor(keysum[:, :], acc[:, 0, :], acc[:, 1, :], ALU.add).then_inc(sum_step, 1)

            def split_sum(u):
                dve.wait_ge(sum_step, u * 2 + 1 + FREE["sum_step"])
                V.tensor_copy(keysum16[:, 0, :], keysum[:, :]).then_inc(sum_step, 1)
                dve.wait_ge(sum_step, u * 2 + 2 + FREE["sum_step"])
                V.tensor_tensor(keysum16[:, 1, :], keysum[:, :], keysum16[:, 0, :],
                                ALU.subtract).then_inc(keysum_ready, 1)

            def sum_output(u, half):
                rows = slice(DK * half, DK * (half + 1))
                dve.wait_ge(o_saved, u + 1 + FREE["o_saved"])
                V.tensor_tensor(oeven[rows, :], oeven[rows, :], oodd[rows, :], ALU.add).then_inc(o_summed, 1)

            def normalise_output(u, half):
                rows = slice(DK * half, DK * (half + 1))
                dve.wait_ge(den_ready, u + 1)
                V.reciprocal(ps[:, SM, 0:BT // 2], ps[:, SM, 0:BT // 2]).then_inc(den_inverted, 1)
                dve.wait_ge(den_inverted, u + 1)
                dve.wait_ge(o_summed, u + 1 + FREE["o_summed"])
                for a in range(2):
                    cols = slice(a * BT // 2, (a + 1) * BT // 2)
                    last = V.tensor_tensor(opair[rows, cols], oeven[rows, cols],
                                           ps[DK * a:DK * (a + 1), SM, 0:BT // 2], ALU.mult)
                last.then_inc(o_normal, 1)

            def add_pair(n, qb):
                dve.wait_ge(wo_ready, n + 1)
                dve.wait_ge(wo_added, n + FREE["wo_added"])
                rows = x[:, bass.ds(qb * TPB, TPB), :]
                V.tensor_tensor(rows, bank(SM).rearrange("p (t c) -> p t c", t=TPB), rows,
                                ALU.add).then_inc(wo_added, 1)

            def pick_weights(k):
                V.tensor_copy(bqp[:, :], bq[:, bass.ds(2 * k, 2)])
                V.tensor_copy(wqp[:, :], wq[:, bass.ds(2 * k * DK, 2 * DK)]).then_inc(wq_ready, 1)

            def low_queries(n, k, halves=(0, 1)):
                dve.wait_ge(qh_ready, 2 * n + 2)
                for half in halves:
                    dst = qhl[DK:2 * DK, bass.ds(2 * k + half, 1), :].rearrange("p o c -> p (o c)")
                    high = qhl[0:DK, bass.ds(2 * k + half, 1), :].rearrange("p o c -> p (o c)")
                    V.scalar_tensor_tensor(dst, ps[DK * half:DK * (half + 1), SM, :], bqp[:, half:half + 1], high,
                                           ALU.add, ALU.subtract).then_inc(ql_ready, 1)

            def head(u, n, prev_half, prev_block, next_head, next_k, last=False):
                m = 0
                for j in range(STEPS):
                    if j == 0 and next_k is not None:
                        dve.wait_ge(ql_ready, 2 * n + 2)
                        pick_weights(next_k)
                    if next_head is not None:
                        for _ in range(MAX_CHUNKS[j]):
                            chunk_max(u + 1, m)
                            m += 1
                    if j == 0 and last:
                        dve.wait_ge(wo_added, (NB - 1) * HEADS // 2 + FREE["wo_added"])
                        for b in range(NB - 1):
                            row_stats(4, b)
                    if j == 5 and last:
                        for b in range(NB - 1):
                            normalise(4, b)
                    if j == 1 and prev_half is not None:
                        finish_sum(u - 1)
                    if j == 2 and prev_half is not None:
                        split_sum(u - 1)
                    if j in (3, 4) and next_k is not None:
                        low_queries(n + 1, next_k, (j - 3,))
                    if j == 3 and prev_block is not None:
                        add_pair(n - 1, prev_block)
                    if j == 6 and next_head is not None:
                        split_max(u + 1)
                    if j == 6 and prev_half is not None:
                        sum_output(u - 1, prev_half)
                        normalise_output(u - 1, prev_half)

            def pair(qb, k, next_qb, next_k, first, last):
                n = qb * (HEADS // 2) + k
                before = None if first else (qb - 1 if isinstance(k, int) and k == 0 else qb)
                head(2 * n, n, None if first else 1, None, 2 * k + 1, next_k)
                head(2 * n + 1, n, 0, before, None if last else 2 * next_k, None, last)

            dve.wait_ge(bo_added, 1)
            pick_weights(0)
            low_queries(0, 0)
            for m in range(NCH):
                chunk_max(0, m)
            split_max(0)
            attention(dve, pair)
            finish_sum(NB * HEADS - 1)
            split_sum(NB * HEADS - 1)
            sum_output(NB * HEADS - 1, 1)
            normalise_output(NB * HEADS - 1, 1)
            add_pair(NB * HEADS // 2 - 1, NB - 1)

            dve.wait_ge(wo_added, NB * HEADS // 2 + FREE["wo_added"])
            row_stats(4, NB - 1)
            normalise(4, NB - 1)
            for n in range(NB):
                dve.wait_ge(b2_added, n + 1)
                dve.wait_ge(fo_psum, n + 1)
                t = slice(n * TPB, (n + 1) * TPB)
                V.tensor_tensor(x[:, t, :], ps[:, 4 + n % 2, :].rearrange("p (t c) -> p t c", t=TPB), x[:, t, :],
                                ALU.add).then_inc(fo_added, 1)

        @block.tensor
        def _(pe):
            mm = nc.tensor.matmul
            pe.sem_inc(m_psum, FREE["m_psum"])
            pe.sem_inc(pv_done, FREE["pv_done"])

            def transpose_xn(k, b, dst=None):
                pe.wait_ge(xn_ready, NB * (k - 1) + b + 1)
                for t in range(TPB):
                    last = nc.tensor.transpose(ps[:, b if dst is None else dst, t * P:(t + 1) * P],
                                               xn[:, TPB * b + t, :], ident[:, :])
                last.then_inc(xnT_psum, 1)

            def tile(i):
                return xnT[:, i * P:(i + 1) * P]

            pe.wait_ge(consts, 1)
            pe.wait_ge(w_first, 16 * 3)
            transpose_xn(1, 0)
            for b in range(NB):
                if b < NB - 1:
                    transpose_xn(1, b + 1)
                pe.wait_ge(xnT_ready, b + 1)
                for i in range(TPB * b, TPB * (b + 1)):
                    if i >= 4:
                        pe.wait_ge(qkv_ready, i - 3)
                    mm(ps[:, 4 + i % 4, 0:3 * P], tile(i), wqkv[:, :], start=True, stop=True).then_inc(qkv_psum, 1)
            def sum_products(i):
                if i > 2:
                    pe.wait_ge(solved, i - 1)
                for s in range(i):
                    if s == 0 and i > 1:
                        pe.wait_ge(kprod_ready, 2 * i - 2)
                    if s == i - 1:
                        pe.wait_ge(kprod_ready, 2 * i - 1)
                    last = mm(ps[:, 4 + i % 2, 0:2 * P], ident[:, :], kprod[1 - i % 2][:, s, :], start=(s == 0),
                              stop=(s == i - 1))
                last.then_inc(kk_summed, 1)

            def sum_updates(i):
                o_bank, q_bank = ps[:, 2 * (i % 2), 0:P], ps[:, 2 * (i % 2) + 1, 0:P]
                if i < 2:
                    pe.wait_ge(xnT_ready, NB)
                else:
                    pe.wait_ge(qo_sbuf, i - 1)
                mm(q_bank, kaq[:, i, 1, :], ident[:, :], start=True, stop=(i == 0)).then_inc(qo_psum, 1)
                for n, s0, s1 in pieces(i):
                    pe.wait_ge(qprod_ready, n)
                    for s in range(s0, s1):
                        mm(o_bank, qprod[:, n % 2, s - s0, 0, :], ident[:, :], start=(s == 0), stop=(s == i - 1))
                        last = mm(q_bank, qprod[:, n % 2, s - s0, 1, :], neg_ident[:, :], start=False,
                                  stop=(s == i - 1))
                    last.then_inc(qprod_used, 1)

            pe.wait_ge(qkv_ready, NT)
            for i in range(1, SUB):
                sum_products(i)
                sum_updates(i - 1)
            sum_updates(SUB - 1)
            pe.wait_ge(qo_sbuf, SUB)

            def operand(b, g, k):
                return sub[:, b, g, k * P:(k + 1) * P]

            def transitions(c, b, gs):
                for g in gs:
                    last = mm(ps[:, b % 2, g * P:(g + 1) * P], operand(b, g, 1), operand(b, g, 2), start=True,
                              stop=True)
                if gs[-1] == RG - 1:
                    last.then_inc(a_psum, 1)

            def additions(b, gs):
                for g in gs:
                    mm(ps[:, 2 + b % 2, g * P:(g + 1) * P], operand(b, g, 2), operand(b, g, 0), start=(g == 0),
                       stop=False, skip_group_check=True)

            def advance(c, b, turn, transitions_follow=True, additions_follow=True):
                pe.wait_ge(a_ready, c + 1)
                pe.wait_ge(y_ready, c - 1 + FREE["y_ready"])
                for g in range(RG):
                    pe.wait_ge(m_ready, c * RG + g + 1)
                    mm(ps[:, 2 + b % 2, g * P:(g + 1) * P], amat[:, b, g, :], mst[:, g, :], start=False,
                       stop=True, skip_group_check=True).then_inc(m_psum, 1)
                    last = mm(ps[:, 4 + b % 2, g * SUB:(g + 1) * SUB], mst[:, g, :],
                              qT[:, :, bass.ds(c * RG + g, 1)].rearrange("p i o -> p (i o)"), start=True, stop=True)
                    if g == RG - 1:
                        last.then_inc(y_psum, 1)
                    if g == 0 and transitions_follow:
                        pe.wait_ge(sub_in[(b + 2) % SLOTS], (turn + (b + 2) // SLOTS + 1) * 16)
                        pe.wait_ge(a_masked, c * 2 + 2)
                    if g < 2 and transitions_follow:
                        transitions(c + 2, (b + 2) % SLOTS, [2 * g, 2 * g + 1])
                    if g >= 2 and additions_follow:
                        additions((b + 1) % SLOTS, [2 * g - 4, 2 * g - 3])

            for c in range(2):
                pe.wait_ge(sub_in[c], 16)
                transitions(c, c, [0, 1, 2, 3])
            additions(0, [0, 1, 2, 3])
            with pe.Fori(0, NRG // SLOTS - 1) as it:
                for b in range(SLOTS):
                    advance(it * SLOTS + b, b, it)
            for b in range(SLOTS):
                advance(NRG - SLOTS + b, b, NRG // SLOTS - 1, b < 2, b < SLOTS - 1)
            pe.wait_ge(y_ready, NRG + FREE["y_ready"])
            pe.wait_ge(w_in, W_REST)
            for b in range(NB):
                for t in range(TPB):
                    last = mm(ps[:, 4 + b, t * P:(t + 1) * P], yT[:, TPB * b + t, :], wproj[:, :], start=True,
                              stop=True)
                last.then_inc(proj_psum, 1)

            transpose_xn(2, 0)
            for b in range(NB):
                if b < NB - 1:
                    transpose_xn(2, b + 1)
                pe.wait_ge(xnT_ready, NB + b + 1)
                for i in range(TPB * b, TPB * (b + 1)):
                    last = mm(ps[:, 4, i * EXPERTS:(i + 1) * EXPERTS], tile(i), gate[:, :], start=True, stop=True)
            last.then_inc(gate_psum, 1)

            def expert_down(e, b, s):
                n = e * NB + b
                pe.wait_ge(hid_ready, n * 2 + 2 + FREE["hid_ready"])
                pe.wait_ge(down_added, n - 1 + FREE["down_added"])
                for t in range(TPB):
                    for j in range(HID // P):
                        last = mm(ps[:, 4 + b % 2, t * P:(t + 1) * P], hidT[:, b % 2, j, t * P:(t + 1) * P],
                                  ew2[:, s, j, :], start=(j == 0), stop=(j == HID // P - 1))
                last.then_inc(down_psum, 1)

            def project(dst, s, which, j, b):
                cols, part = slice(BT * b, BT * (b + 1)), slice(j * P, (j + 1) * P)
                mm(dst, whigh[:, s, which, part], xhigh[:, cols], start=True, stop=False)
                mm(dst, whigh[:, s, which, part], xlow[:, cols], start=False, stop=False)
                return mm(dst, wlow[:, s, which, part], xhigh[:, cols], start=False, stop=True)

            pe.wait_ge(xlow_ready, NB)
            def two_experts(ep, first=False):
                for s in range(2):
                    e = ep * 2 + s
                    pe.wait_ge(ew_in[s], ep * 48 + 48)
                    pe.wait_ge(ew_split, e + 1)
                    for n in range(UP):
                        b, j = n // 2, n % 2
                        pe.wait_ge(act1_ready, e * UP + n - 1 + FREE["act1_ready"])
                        project(bank(2 * j), s, 0, j, b).then_inc(up_psum, 1)
                        pe.wait_ge(hid_ready, e * UP + n - 1 + FREE["hid_ready"])
                        project(bank(2 * j + 1), s, 1, j, b).then_inc(gt_psum, 1)
                        if j == 0 and n > 0:
                            expert_down(e, b - 1, s)
                        elif n == 0 and not (first and s == 0):
                            expert_down(e - 1, NB - 1, 1 - s)

            two_experts(0, first=True)
            with pe.Fori(1, EXPERTS // 2) as ep:
                two_experts(ep)
            expert_down(EXPERTS - 1, NB - 1, 1)

            for b in range(NB):
                transpose_xn(3, b)
            for b in range(NB):
                pe.wait_ge(xnT_ready, 2 * NB + b + 1)
                mm(bank(b), wk2[:, :, :].rearrange("p a d -> p (a d)"), xnT[:, BT * b:BT * (b + 1)], start=True,
                   stop=True).then_inc(kp_psum, 1)
            for n in range(2):
                for t in range(8):
                    last = mm(ps[:, 4 + n, t * DK:(t + 1) * DK], tile(8 * n + t), wv[:, :], start=True, stop=True)
                last.then_inc(vp_psum, 1)
            pe.wait_ge(kl_ready, NB)
            pe.wait_ge(v_ready, 2)
            pe.wait_ge(klm_ones, 2)

            def scores(u, h, j, a):
                keys = slice((2 * j + a) * P, (2 * j + a + 1) * P)
                dst = bank(2 * (j % 2) + a)
                pe.wait_ge(p_ready, u * STEPS + j - 1 + FREE["p_ready"])
                mm(dst, khh[:, keys], qhl[:, bass.ds(h, 1), :].rearrange("p o c -> p (o c)"), start=True, stop=False)
                last = mm(dst, klm[:, keys], qhm[:, bass.ds(h, 1), :].rearrange("p o c -> p (o c)"), start=False,
                          stop=True)
                if a == 1:
                    last.then_inc(st_ready, 1)

            def max_scores(u, h, m, pairs_ready):
                if m == 0:
                    pe.wait_ge(ql_ready, pairs_ready)
                pe.wait_ge(mx_free, u * NCH + m - 1 + FREE["mx_free"])
                qt, kb = m // NB, m % NB
                mm(bank(MX + m % 2), qhl[:, bass.ds(h, 1), qt * P:(qt + 1) * P].rearrange("p o c -> p (o c)"),
                   khh[:, kb * BT:(kb + 1) * BT], start=True, stop=True).then_inc(mx_ready, 1)

            def turn_max(u):
                pe.wait_ge(rowmax_ready, u + 1)
                for qt in range(TPB):
                    last = nc.tensor.transpose(small16[DK:DK + 2, qt * P:(qt + 1) * P], m16[:, qt, :], ident16[:, :])
                last.then_inc(tr_ready, 1)

            def weigh_values(u, j):
                pe.wait_ge(p_ready, u * STEPS + j + 1 + FREE["p_ready"])
                if j == 0:
                    pe.wait_ge(o_saved, u + FREE["o_saved"])
                for a in range(2):
                    last = mm(ps[DK * a:DK * (a + 1), OB, :], vt[:, 2 * j + a, :], pr[:, j % 4, a, :], start=(j == 0),
                              stop=(j == STEPS - 1))
                last.then_inc(pv_done, 1)

            def denominator(u, pairs_added, pairs_made=None):
                pe.wait_ge(keysum_ready, u + 1)
                pe.wait_ge(o_normal, u + FREE["o_normal"])
                pe.wait_ge(wo_added, pairs_added + FREE["wo_added"])
                if pairs_made is not None:
                    pe.wait_ge(ql_ready, 2 * pairs_made)
                for part in range(2):
                    for a in range(2):
                        cols = slice(a * BT // 2, (a + 1) * BT // 2)
                        last = mm(ps[DK * a:DK * (a + 1), SM, 0:BT // 2], ones16[:, :], keysum16[:, part, cols],
                                  start=(part == 0), stop=(part == 1))
                last.then_inc(den_ready, 1)

            def project_pair(n, k):
                pe.wait_ge(o_normal, 2 * n + 2 + FREE["o_normal"])
                for t in range(TPB):
                    last = mm(ps[:, SM, t * P:(t + 1) * P], opair[:, t * P:(t + 1) * P],
                              wo[:, bass.ds(k, 1), :].rearrange("p o c -> p (o c)"), start=True, stop=True)
                last.then_inc(wo_ready, 1)

            def make_queries(n, qb):
                pe.wait_ge(wq_ready, n + 1)
                pe.wait_ge(o_normal, 2 * n - 3 + FREE["o_normal"])
                mm(bank(SM), wqp[:, :], xnT[:, bass.ds(qb * BT, BT)], start=True, stop=True).then_inc(q_psum, 1)

            def head(u, h, even, prev, prev_pair, next_head, ready, n, next_qb):
                m = 0
                nxt = next_head is not None
                for j in range(STEPS):
                    if j == 0:
                        pe.wait_ge(t2_ready, u + 1)
                        pe.wait_ge(qm_copied, u + 1)
                    chunks = list(range(m, m + MAX_CHUNKS[j])) if nxt else []
                    m += len(chunks)
                    if j == 7 and nxt:
                        turn_max(u + 1)
                    scores(u, h, j, 0)
                    if chunks:
                        max_scores(u + 1, next_head, chunks[0], ready)
                    scores(u, h, j, 1)
                    if chunks:
                        max_scores(u + 1, next_head, chunks[1], ready)
                    if j > 0:
                        weigh_values(u, j - 1)
                    elif prev:
                        weigh_values(u - 1, STEPS - 1)
                    if len(chunks) > 2:
                        max_scores(u + 1, next_head, chunks[2], ready)
                    if j == 1 and next_qb is not None:
                        make_queries(n + 1, next_qb)
                    if j == 1 and prev_pair is not None:
                        project_pair(n - 1, prev_pair)
                    if j == 5 and prev:
                        denominator(u - 1, n - 1 if even else n if prev_pair is not None else 0,
                                    n + 2 if next_qb is not None else None)

            def pair(qb, k, next_qb, next_k, first, last):
                n = qb * (HEADS // 2) + k
                before = None if first else (HEADS // 2 - 1 if isinstance(k, int) and k == 0 else k - 1)
                head(2 * n, 2 * k, True, not first, None, 2 * k + 1, 2 * n + 2, n, next_qb)
                head(2 * n + 1, 2 * k + 1, False, True, before, None if last else 2 * next_k, 2 * n + 4, n, None)

            pe.wait_ge(wq_ready, 1)
            pe.wait_ge(v_ready, 2)
            mm(bank(SM), wqp[:, :], xnT[:, 0:BT], start=True, stop=True).then_inc(q_psum, 1)
            for m in range(NCH):
                max_scores(0, 0, m, 2)
            turn_max(0)
            attention(pe, pair)
            weigh_values(NB * HEADS - 1, STEPS - 1)
            pe.wait_ge(p_ready, NB * HEADS * STEPS + FREE["p_ready"])
            for b in range(NB - 1):
                transpose_xn(4, b)
            denominator(NB * HEADS - 1, NB * HEADS // 2 - 1)
            project_pair(NB * HEADS // 2 - 1, HEADS // 2 - 1)

            for n in range(NB):
                if n == 1:
                    transpose_xn(4, NB - 1, OB)
                pe.wait_ge(xnT_ready, 3 * NB + (NB - 1 if n == 0 else n + 1))
                for j in range(NF):
                    pe.wait_ge(ff_ready, n * NF + j - 3 + FREE["ff_ready"])
                    mm(bank(j), w1[:, j * P:(j + 1) * P], xnT[:, n * BT:(n + 1) * BT], start=True,
                       stop=True).then_inc(ff_psum, 1)
                pe.wait_ge(ff_ready, n * NF + NF + FREE["ff_ready"])
                pe.wait_ge(fo_added, n - 1 + FREE["fo_added"])
                for t in range(TPB):
                    for j in range(NF):
                        last = mm(ps[:, 4 + n % 2, t * P:(t + 1) * P], ffT[:, n % 2, j, t * P:(t + 1) * P],
                                  w2[:, j, :], start=(j == 0), stop=(j == NF - 1))
                last.then_inc(fo_psum, 1)


def kernel(**inputs):
    import numpy as np
    import concourse.bacc as bacc
    from concourse.bass_utils import run_bass_kernel_spmd

    g = {name: np.asarray(a) for name, a in inputs.items()}
    arrays = {
        "x": g["L0_attn_x"],
        "wqkv": np.concatenate([g["L0_attn_Wq"].T, g["L0_attn_Wk"].T, g["L0_attn_Wv"].T], axis=1),
        "wproj": g["L0_attn_Wproj"].T,
        "alpha": g["L0_attn_alpha_raw"], "beta": g["L0_attn_beta_raw"],
        "gate": g["L0_ffn_gate_w"].T, "ew1": g["L0_ffn_w1"], "ew2": g["L0_ffn_w2"], "ew3": g["L0_ffn_w3"],
        "wq": g["L1_attn_Wq"], "bq": g["L1_attn_bq"].reshape(HEADS, DK).T,
        "wk": g["L1_attn_Wk"], "bk": g["L1_attn_bk"].reshape(DK, 1),
        "wv": g["L1_attn_Wv"], "bv": g["L1_attn_bv"], "wo": g["L1_attn_Wo"], "bo": g["L1_attn_bo"],
        "w1": g["L1_ffn_W1"], "b1": g["L1_ffn_b1"].reshape(FF // P, P).T,
        "w2": g["L1_ffn_W2"], "b2": g["L1_ffn_b2"],
    }
    arrays = {name: np.ascontiguousarray(a) for name, a in arrays.items()}
    nc = bacc.Bacc("TRN2", target_bir_lowering=False, num_devices=1)
    io = {name: nc.dram_tensor("in_" + name, a.shape, mybir.dt.from_np(a.dtype), kind="ExternalInput").ap()
          for name, a in arrays.items()}
    shape = arrays["x"].shape
    out = nc.dram_tensor("out", shape, F32, kind="ExternalOutput").ap()
    build(nc, io, out)
    result = run_bass_kernel_spmd(nc, [{"in_" + name: a for name, a in arrays.items()}], core_ids=[0])
    return result.results[0]["out"]
```
